# Optimizing a Trainium2 kernel written in Bass

```python
import numpy as np
import jax
import jax.numpy as jnp

def _softmax(x, axis=-1):
    return jax.nn.softmax(x, axis=axis)

def _gelu(x):
    return jax.nn.gelu(x, approximate=True)

def _silu(x):
    return jax.nn.silu(x)

def _sigmoid(x):
    return jax.nn.sigmoid(x)

def _layernorm(x, axis=-1, eps=1e-05):
    m = jnp.mean(x, axis=axis, keepdims=True)
    v = jnp.var(x, axis=axis, keepdims=True)
    return (x - m) / jnp.sqrt(v + eps)

def _scatter_add(tgt, idx, src, axis=0):
    return tgt.at[idx].add(src)

def _segment_sum(src, seg, n):
    return jax.ops.segment_sum(src, seg, n)
kernel_name = 'mk_sandwich_d1_jaxref_r8_37d751'

def setup_inputs(seed: int=0):
    np.random.seed(seed)
    _w = jnp.asarray

    def _L0_attn_setup():
        import jax, jax.numpy as jnp
        import numpy as np
        import math
        from jax import lax
        B, L, D = (8, 512, 128)
        FILTER_ORDER = 64
        EMB_DIM = 3
        SHIFT = 0.05
        KSIZE = 3

        def _implicit_filter(f_w1, f_b1, freq1, f_w2, f_b2, freq2, f_w3, f_b3, freq3, f_wout):
            t = jnp.linspace(0.0, 1.0, L)
            t_resc = jnp.linspace(0.0, L - 1.0, L)
            w = 2.0 * jnp.pi * t_resc / L
            bands = (EMB_DIM - 1) // 2
            f = jnp.linspace(0.0001, bands - 1.0, bands)
            fw = f[None, :] * w[:, None]
            z = jnp.concatenate([t[:, None], jnp.cos(fw), -jnp.sin(fw)], axis=-1)
            h = jnp.sin(freq1 * (z @ f_w1 + f_b1))
            h = jnp.sin(freq2 * (h @ f_w2 + f_b2))
            h = jnp.sin(freq3 * (h @ f_w3 + f_b3))
            h = h @ f_wout
            max_decay = math.log(0.01) / 0.3
            min_decay = math.log(0.01) / 1.5
            deltas = jnp.linspace(min_decay, max_decay, D)
            decay = jnp.exp(-t[:, None] * jnp.abs(deltas)[None, :])
            return h * (decay + SHIFT)
        key = jax.random.key(seed)
        ks = jax.random.split(key, 12)
        s = 0.02
        return {'u': jax.random.normal(ks[0], (B, L, D), jnp.float32), 'w_in': jax.random.normal(ks[1], (D, 3 * D), jnp.float32) * s, 'b_in': jnp.zeros((3 * D,), jnp.float32), 'sf_w': jax.random.normal(ks[2], (3 * D, KSIZE), jnp.float32) * 0.3, 'sf_b': jnp.zeros((3 * D,), jnp.float32), 'f_w1': jax.random.normal(ks[3], (EMB_DIM, FILTER_ORDER), jnp.float32) * 0.5, 'f_b1': jnp.zeros((FILTER_ORDER,), jnp.float32), 'freq1': jnp.ones((FILTER_ORDER,), jnp.float32), 'f_w2': jax.random.normal(ks[4], (FILTER_ORDER, FILTER_ORDER), jnp.float32) * 0.12, 'f_b2': jnp.zeros((FILTER_ORDER,), jnp.float32), 'freq2': jnp.ones((FILTER_ORDER,), jnp.float32), 'f_w3': jax.random.normal(ks[5], (FILTER_ORDER, FILTER_ORDER), jnp.float32) * 0.12, 'f_b3': jnp.zeros((FILTER_ORDER,), jnp.float32), 'freq3': jnp.ones((FILTER_ORDER,), jnp.float32), 'f_wout': jax.random.normal(ks[6], (FILTER_ORDER, D), jnp.float32) * s, 'filt_bias': jax.random.normal(ks[7], (D,), jnp.float32), 'w_out': jax.random.normal(ks[8], (D, D), jnp.float32) * s, 'b_out': jnp.zeros((D,), jnp.float32)}
    _L0_attn_in = _L0_attn_setup()

    def _L0_ffn_setup():
        import jax, jax.numpy as jnp
        import numpy as np
        B, S, D, F, E, K = (4, 256, 128, 512, 4, 2)
        key = jax.random.key(seed)
        k = jax.random.split(key, 6)
        x = jax.random.normal(k[0], (B, S, D), jnp.float32)
        router_w = jax.random.normal(k[1], (D, E), jnp.float32) * D ** (-0.5)
        router_b = jnp.zeros((E,), jnp.float32)
        w1 = jax.random.normal(k[2], (E, D, F), jnp.float32) * 0.02
        w3 = jax.random.normal(k[3], (E, D, F), jnp.float32) * 0.02
        w2 = jax.random.normal(k[4], (E, F, D), jnp.float32) * 0.02
        return {'x': x, 'router_w': router_w, 'router_b': router_b, 'w1': w1, 'w3': w3, 'w2': w2}
    _L0_ffn_in = _L0_ffn_setup()
    _d = {'L0_attn_u': _L0_attn_in['u'], 'L0_attn_w_in': _L0_attn_in['w_in'], 'L0_attn_b_in': _L0_attn_in['b_in'], 'L0_attn_sf_w': _L0_attn_in['sf_w'], 'L0_attn_sf_b': _L0_attn_in['sf_b'], 'L0_attn_f_w1': _L0_attn_in['f_w1'], 'L0_attn_f_b1': _L0_attn_in['f_b1'], 'L0_attn_freq1': _L0_attn_in['freq1'], 'L0_attn_f_w2': _L0_attn_in['f_w2'], 'L0_attn_f_b2': _L0_attn_in['f_b2'], 'L0_attn_freq2': _L0_attn_in['freq2'], 'L0_attn_f_w3': _L0_attn_in['f_w3'], 'L0_attn_f_b3': _L0_attn_in['f_b3'], 'L0_attn_freq3': _L0_attn_in['freq3'], 'L0_attn_f_wout': _L0_attn_in['f_wout'], 'L0_attn_filt_bias': _L0_attn_in['filt_bias'], 'L0_attn_w_out': _L0_attn_in['w_out'], 'L0_attn_b_out': _L0_attn_in['b_out'], 'L0_ffn_router_w': _L0_ffn_in['router_w'], 'L0_ffn_router_b': _L0_ffn_in['router_b'], 'L0_ffn_w1': _L0_ffn_in['w1'], 'L0_ffn_w3': _L0_ffn_in['w3'], 'L0_ffn_w2': _L0_ffn_in['w2']}
    _x0 = _d['L0_attn_u']
    _d['L0_attn_u'] = jax.random.normal(jax.random.fold_in(jax.random.key(seed), 1), (8, 256, 128), dtype=_x0.dtype)
    del _x0
    return _d

def reference(L0_attn_u, L0_attn_w_in, L0_attn_b_in, L0_attn_sf_w, L0_attn_sf_b, L0_attn_f_w1, L0_attn_f_b1, L0_attn_freq1, L0_attn_f_w2, L0_attn_f_b2, L0_attn_freq2, L0_attn_f_w3, L0_attn_f_b3, L0_attn_freq3, L0_attn_f_wout, L0_attn_filt_bias, L0_attn_w_out, L0_attn_b_out, L0_ffn_router_w, L0_ffn_router_b, L0_ffn_w1, L0_ffn_w3, L0_ffn_w2):

    def _L0_attn_ref(u, w_in, b_in, sf_w, sf_b, f_w1, f_b1, freq1, f_w2, f_b2, freq2, f_w3, f_b3, freq3, f_wout, filt_bias, w_out, b_out):
        import jax, jax.numpy as jnp
        import numpy as np
        import math
        from jax import lax
        B, L, D = (8, 512, 128)
        FILTER_ORDER = 64
        EMB_DIM = 3
        SHIFT = 0.05
        KSIZE = 3

        def _implicit_filter(f_w1, f_b1, freq1, f_w2, f_b2, freq2, f_w3, f_b3, freq3, f_wout):
            t = jnp.linspace(0.0, 1.0, L)
            t_resc = jnp.linspace(0.0, L - 1.0, L)
            w = 2.0 * jnp.pi * t_resc / L
            bands = (EMB_DIM - 1) // 2
            f = jnp.linspace(0.0001, bands - 1.0, bands)
            fw = f[None, :] * w[:, None]
            z = jnp.concatenate([t[:, None], jnp.cos(fw), -jnp.sin(fw)], axis=-1)
            h = jnp.sin(freq1 * (z @ f_w1 + f_b1))
            h = jnp.sin(freq2 * (h @ f_w2 + f_b2))
            h = jnp.sin(freq3 * (h @ f_w3 + f_b3))
            h = h @ f_wout
            max_decay = math.log(0.01) / 0.3
            min_decay = math.log(0.01) / 1.5
            deltas = jnp.linspace(min_decay, max_decay, D)
            decay = jnp.exp(-t[:, None] * jnp.abs(deltas)[None, :])
            return h * (decay + SHIFT)
        b, l, d = u.shape
        up = (u @ w_in + b_in).transpose(0, 2, 1)
        uc = lax.conv_general_dilated(up, sf_w[:, None, :], (1,), [(KSIZE - 1, KSIZE - 1)], feature_group_count=3 * d, dimension_numbers=('NCH', 'OIH', 'NCH'))[..., :l] + sf_b[None, :, None]
        x0, x1, v = jnp.split(uc, 3, axis=1)
        k = _implicit_filter(f_w1, f_b1, freq1, f_w2, f_b2, freq2, f_w3, f_b3, freq3, f_wout).T
        v = v * x1
        n = 2 * l
        y = jnp.fft.irfft(jnp.fft.rfft(v, n=n) * jnp.fft.rfft(k, n=n), n=n)[..., :l]
        v = y + v * filt_bias[None, :, None]
        out = (v * x0).transpose(0, 2, 1)
        return out @ w_out + b_out

    def _L0_ffn_ref(x, router_w, router_b, w1, w3, w2):
        import jax, jax.numpy as jnp
        import numpy as np
        B, S, D, F, E, K = (4, 256, 128, 512, 4, 2)
        b, s, d = x.shape
        T = b * s
        e = router_w.shape[1]
        xf = x.reshape(T, d)
        logits = xf @ router_w + router_b
        probs = jax.nn.softmax(logits, axis=-1)
        top_p, top_i = jax.lax.top_k(probs, K)
        top_p = top_p / jnp.sum(top_p, axis=-1, keepdims=True)
        gates = jnp.zeros((T, e), xf.dtype).at[jnp.arange(T)[:, None], top_i].add(top_p)
        h = jax.nn.silu(jnp.einsum('td,edf->etf', xf, w1)) * jnp.einsum('td,edf->etf', xf, w3)
        expert_out = jnp.einsum('etf,efd->etd', h, w2)
        out = jnp.einsum('te,etd->td', gates, expert_out)
        return out.reshape(b, s, d)
    x = L0_attn_u
    x = x + _layernorm(_L0_attn_ref(_layernorm(x, axis=-1), L0_attn_w_in, L0_attn_b_in, L0_attn_sf_w, L0_attn_sf_b, L0_attn_f_w1, L0_attn_f_b1, L0_attn_freq1, L0_attn_f_w2, L0_attn_f_b2, L0_attn_freq2, L0_attn_f_w3, L0_attn_f_b3, L0_attn_freq3, L0_attn_f_wout, L0_attn_filt_bias, L0_attn_w_out, L0_attn_b_out), axis=-1)
    x = x + _layernorm(_L0_ffn_ref(_layernorm(x, axis=-1), L0_ffn_router_w, L0_ffn_router_b, L0_ffn_w1, L0_ffn_w3, L0_ffn_w2), axis=-1)
    return x

_drawn_inputs = setup_inputs


def setup_inputs(seed=0):
    import zlib

    import numpy as np

    out = dict(_drawn_inputs(seed))
    spreads = {'L0_attn_b_in': (0.0, 0.1),
     'L0_attn_sf_b': (0.0, 0.1),
     'L0_attn_f_b1': (0.0, 0.36),
     'L0_attn_freq1': (1.0, 0.6),
     'L0_attn_f_b2': (0.0, 0.1),
     'L0_attn_freq2': (1.0, 0.6),
     'L0_attn_f_b3': (0.0, 0.32),
     'L0_attn_freq3': (1.0, 0.6),
     'L0_attn_b_out': (0.0, 0.1),
     'L0_ffn_router_b': (0.0, 0.1)}
    factors = {}
    for name, (base, spread) in spreads.items():
        noise = np.random.default_rng([zlib.crc32(name.encode()), seed]).standard_normal(out[name].shape)
        drawn = base * np.exp(spread * noise) if base else spread * noise
        out[name] = jnp.asarray(drawn.astype(out[name].dtype))
    for name, factor in factors.items():
        out[name] = (out[name] * factor).astype(out[name].dtype)
    return out
```

```python
from contextlib import ExitStack

import numpy as np

import concourse.bass as bass
from concourse import mybir

F32 = mybir.dt.float32
F32R = mybir.dt.float32r
ALU = mybir.AluOpType
ACT = mybir.ActivationFunctionType
AX_X = mybir.AxisListType.X

P = 128
LFILT = 512
NEXP = 4
HID = 512
FT = HID // P
TILES = 4
CHUNK = TILES * P
SEQ = 256
BPC = CHUNK // SEQ
STEPS = NEXP * FT
EPS = 1e-5
TWO_PI = 2.0 * np.pi
TWO_PI_HI = 6.28125
ROUND = 1.5 * 2.0 ** 23
PI_BELOW = 3.1415925

C_BIN, C_SFW, C_SFB, C_FB, C_FF, C_RB, NCOL = 0, 3, 12, 15, 18, 21, 25
X0, X1, V = 0, 1, 2


def build(nc, x, w_in, w_out, cols, rows, filt_z, filt_mats, decay, router, w1, w3, w2,
          fwd, inv, ident, tri, out):
    ntok = x.shape[0]
    NCH = ntok // CHUNK
    NG = NCH * STEPS

    with ExitStack() as ctx:
        def sb(name, shape, dt=F32):
            return ctx.enter_context(nc.sbuf_tensor(name, shape, dt))

        def ps(name, shape=(P, 512)):
            return ctx.enter_context(nc.psum_tensor(name, list(shape), F32))

        def sem(name):
            return ctx.enter_context(nc.semaphore(name))

        x_sb = sb("x_sb", [P, NCH * TILES, P])
        cols_sb = sb("cols_sb", [P, NCOL])
        rows_sb = sb("rows_sb", [1, 5 * P])
        rows_hi = sb("rows_hi", [1, 4 * P], F32R)
        rows_lo = sb("rows_lo", [1, 4 * P], F32R)
        ones_row = sb("ones_row", [1, P])
        ones_r = sb("ones_r", [1, P], F32R)
        filt_z_sb = sb("filt_z_sb", [6, P + SEQ])
        filt_mats_sb = sb("filt_mats_sb", [P, 3, P])
        decay_sb = sb("decay_sb", [P, 4, P])
        ident_sb = sb("ident_sb", [P, P])
        tri_sb = sb("tri_sb", [P, NEXP * NEXP])
        fwd_sb = sb("fwd_sb", [P, 2, 2, LFILT], F32R)
        inv_sb = sb("inv_sb", [P, 2, 4, SEQ], F32R)
        w_in_sb = sb("w_in_sb", [P, 3 * P])
        w_in_hi = sb("w_in_hi", [P, 3 * P], F32R)
        w_in_lo = sb("w_in_lo", [P, 3 * P], F32R)
        w_out_sb = sb("w_out_sb", [P, P])
        w_out_hi = sb("w_out_hi", [P, P], F32R)
        w_out_lo = sb("w_out_lo", [P, P], F32R)
        router_sb = sb("router_sb", [P, NEXP])
        router_hl = sb("router_hl", [P, 2 * NEXP], F32R)
        EW_RING = 6
        ew_sb = [sb(f"ew_sb{i}", [P, HID]) for i in range(EW_RING)]
        ew_hi = [sb(f"ew{n}_hi", [P, NEXP, HID], F32R) for n in (1, 3, 2)]
        ew_lo = [sb(f"ew{n}_lo", [P, NEXP, HID], F32R) for n in (1, 3, 2)]
        tap2_bias = sb("tap2_bias", [P, 3])
        minus_half = sb("minus_half", [P, TILES])
        e_base = sb("e_base", [P, TILES * NEXP])

        khat_a = sb("khat_a", [P, 4, BPC, P])
        khat_b = sb("khat_b", [P, 4, BPC, P])

        kinds = ("x", "o", "x1", "moe")
        stats = {k: sb(f"stats_{k}", [P, TILES, 6]) for k in kinds}
        mv = {k: sb(f"mv_{k}", [P, TILES, 2]) for k in kinds}
        veps = {k: sb(f"veps_{k}", [P, TILES]) for k in kinds}
        rstd = {k: sb(f"rstd_{k}", [P, TILES]) for k in kinds}
        negm = {k: sb(f"negm_{k}", [P, TILES]) for k in ("o", "moe")}
        nbias = {k: sb(f"nbias_{k}", [P, TILES]) for k in ("o", "moe")}
        xn = sb("xn", [P, TILES, P])
        xnT_hi = sb("xnT_hi", [P, CHUNK], F32R)
        xnT_lo = sb("xnT_lo", [P, CHUNK], F32R)
        up = [sb(f"up{s}", [P, BPC, SEQ + 2]) for s in range(3)]
        tap2 = [sb(f"tap2_{s}", [P, BPC, SEQ]) for s in range(3)]
        uc = tap2
        vx = sb("vx", [P, BPC, SEQ])
        vT_hi = sb("vT_hi", [P, 2, BPC, P], F32R)
        vT_lo = sb("vT_lo", [P, 2, BPC, P], F32R)
        pa = sb("pa", [P, 2, 2, BPC * P])
        pb = sb("pb", [P, 2, 2, BPC * P])
        yh = pa
        yh_hi = sb("yh_hi", [P, 2, 2, BPC * P], F32R)
        yh_lo = sb("yh_lo", [P, 2, 2, BPC * P], F32R)
        gated = sb("gated", [P, CHUNK])
        gated_hi = sb("gated_hi", [P, CHUNK], F32R)
        gated_lo = sb("gated_lo", [P, CHUNK], F32R)
        o_n = sb("o_n", [P, TILES, P])
        x1 = sb("x1", [P, 2, TILES, P])
        xf = xn
        xfT_hi = sb("xfT_hi", [P, 2, CHUNK], F32R)
        xfT_lo = sb("xfT_lo", [P, 2, CHUNK], F32R)

        lg_a = sb("lg_a", [P, TILES, NEXP])
        lg = sb("lg", [P, TILES, NEXP])
        lg_max = sb("lg_max", [P, TILES])
        lg_z = sb("lg_z", [P, TILES, NEXP])
        ge = sb("ge", [P, TILES, NEXP])
        beats = sb("beats", [P, TILES, NEXP, NEXP])
        ties = sb("ties", [P, TILES, NEXP, NEXP])
        ties_low = sb("ties_low", [P, TILES, NEXP, NEXP])
        ahead = sb("ahead", [P, TILES, NEXP, NEXP])
        place = sb("place", [P, TILES, NEXP])
        kept = sb("kept", [P, TILES, NEXP])
        ksum = sb("ksum", [P, TILES])
        krec = sb("krec", [P, TILES])
        gates = sb("gates", [P, 2, TILES, NEXP])

        silu = sb("silu", [P, 2, CHUNK])
        hid = sb("hid", [P, 2, CHUNK])
        hid_hi = sb("hid_hi", [P, 4, CHUNK], F32R)
        hid_lo = sb("hid_lo", [P, 4, CHUNK], F32R)
        farg, fturn, fred, fh = (hid[:, i // 2, (i % 2) * SEQ:(i % 2 + 1) * SEQ] for i in range(4))
        taps = silu[:, 0].rearrange("p (i d) -> p i d", i=4)
        fold, fold_hi, fold_lo = (t.rearrange("p (h n) -> p h n", h=2)
                                  for t in (silu[:, 1], hid_hi[:, 0], hid_lo[:, 0]))
        eoT = sb("eoT", [P, CHUNK])
        acc = sb("acc", [P, TILES, P])
        acc_n = sb("acc_n", [P, TILES, P])
        y = acc_n

        ps_h1 = [ps("ps_h1a"), ps("ps_h1b")]
        ps_h3 = [ps("ps_h3a"), ps("ps_h3b")]
        ps_eo = ps("ps_eo")
        ps_et = ps("ps_et")
        ps_a = ps("ps_a")
        ps_b = ps("ps_b")

        ld_x = [sem(f"ld_x{c}") for c in range(NCH)]
        ld = {k: sem(f"ld_{k}") for k in ("cols", "rows", "fz", "fmats", "decay", "ident", "tri",
                                         "w_in", "w_out", "router", "fwd", "inv")}
        ld_ew = [[sem(f"ld_ew{m}_{e}") for e in range(NEXP)] for m in range(3)]
        stored = sem("stored")
        consts_set = sem("consts_set")
        pads_set = sem("pads_set")
        ew_hi_done = sem("ew_hi_done")
        ew_lo_done = sem("ew_lo_done")
        w_in_hi_done = sem("w_in_hi_done")
        w_in_lo_done = sem("w_in_lo_done")
        w_out_hi_done = sem("w_out_hi_done")
        w_out_lo_done = sem("w_out_lo_done")
        tap2_bias_a = sem("tap2_bias_a")
        tap2_bias_done = sem("tap2_bias_done")
        f_mm = sem("f_mm")
        f_step = sem("f_step")
        f_red = sem("f_red")
        f_sin = sem("f_sin")
        taps_mm = sem("taps_mm")
        taps_done = sem("taps_done")
        fold_done = sem("fold_done")
        fold_hi_done = sem("fold_hi_done")
        fold_lo_done = sem("fold_lo_done")
        khat_mm = sem("khat_mm")
        khat_copied = sem("khat_copied")
        khat_zeroed = sem("khat_zeroed")
        ln_stats = {k: sem(f"ln_stats_{k}") for k in kinds}
        ln_mv = {k: sem(f"ln_mv_{k}") for k in kinds}
        ln_veps = {k: sem(f"ln_veps_{k}") for k in kinds}
        ln_rstd = {k: sem(f"ln_rstd_{k}") for k in kinds}
        ln_nbias = {k: sem(f"ln_nbias_{k}") for k in ("o", "moe")}
        xn_done = sem("xn_done")
        xnT_mm = sem("xnT_mm")
        xnT_hi_done = sem("xnT_hi_done")
        xnT_lo_done = sem("xnT_lo_done")
        proj_mm = [sem(f"proj_mm{s}") for s in range(3)]
        up_done = [sem(f"up_done{s}") for s in range(3)]
        tap2_done = [sem(f"tap2_done{s}") for s in range(3)]
        tap1_done = [sem(f"tap1_done{s}") for s in range(3)]
        uc_done = [sem(f"uc_done{s}") for s in range(3)]
        vx_done = sem("vx_done")
        vT_mm = sem("vT_mm")
        vT_hi_done = sem("vT_hi_done")
        vT_lo_done = sem("vT_lo_done")
        fwd_mm = [sem("fwd_mm_even"), sem("fwd_mm_odd")]
        prod_a = [sem("prod_a_even"), sem("prod_a_odd")]
        prod_b = [sem("prod_b_even"), sem("prod_b_odd")]
        yh_done = [sem("yh_done_even"), sem("yh_done_odd")]
        yh_hi_done = [sem("yh_hi_even"), sem("yh_hi_odd")]
        yh_lo_done = [sem("yh_lo_even"), sem("yh_lo_odd")]
        y_mm = sem("y_mm")
        gated_done = sem("gated_done")
        gated_hi_done = sem("gated_hi_done")
        gated_lo_done = sem("gated_lo_done")
        o_mm = sem("o_mm")
        o_n_done = sem("o_n_done")
        x1_done = sem("x1_done")
        xf_done = sem("xf_done")
        xfT_mm = sem("xfT_mm")
        xfT_hi_done = sem("xfT_hi_done")
        xfT_lo_done = sem("xfT_lo_done")
        router_hi_done = sem("router_hi_done")
        router_lo_done = sem("router_lo_done")
        logits_mm = sem("logits_mm")
        lg_a_done = sem("lg_a_done")
        lg_done = sem("lg_done")
        lg_max_done = sem("lg_max_done")
        lg_z_done = sem("lg_z_done")
        ge_done = sem("ge_done")
        beats_done = sem("beats_done")
        ties_done = sem("ties_done")
        ties_low_done = sem("ties_low_done")
        ahead_done = sem("ahead_done")
        place_done = sem("place_done")
        kept_done = sem("kept_done")
        ksum_done = sem("ksum_done")
        krec_done = sem("krec_done")
        gates_done = sem("gates_done")
        h1_mm = sem("h1_mm")
        h3_mm = sem("h3_mm")
        silu_done = sem("silu_done")
        hid_done = sem("hid_done")
        hid_hi_done = sem("hid_hi_done")
        hid_lo_done = sem("hid_lo_done")
        eo_mm = sem("eo_mm")
        eoT_done = sem("eoT_done")
        et_mm = sem("et_mm")
        acc_done = sem("acc_done")
        acc_n_done = sem("acc_n_done")
        y_done = sem("y_done")

        block = ctx.enter_context(nc.Block())

        x_dram = x.rearrange("(t p) d -> p t d", p=P)
        out_dram = out.rearrange("(t p) d -> p t d", p=P)
        ew_dram = [w1.rearrange("e d f -> d e f"), w3.rearrange("e d f -> d e f"),
                   w2.rearrange("e (j f) d -> f e j d", f=P)]

        FIRST, LAST = -STEPS, NG + 6

        def hyena_at(g):
            c, stage = (g + STEPS) // STEPS, g % STEPS
            return (c, stage) if c < NCH else (c, None)

        @block.sync
        def _(sp):
            sp.dma_start(x_sb[:, 0:TILES, :], x_dram[:, 0:TILES, :]).then_inc(ld_x[0], 16)
            sp.dma_start(filt_z_sb[:], filt_z).then_inc(ld["fz"], 16)
            sp.dma_start(filt_mats_sb[:], filt_mats).then_inc(ld["fmats"], 16)
            sp.dma_start(decay_sb[:], decay).then_inc(ld["decay"], 16)
            for e in range(NEXP):
                for m in range(3):
                    i = 3 * e + m
                    dst = ew_sb[i % EW_RING][:]
                    src = ew_dram[m][:, e]
                    if i >= EW_RING:
                        sp.wait_ge(ew_lo_done, i - EW_RING + 1)
                    if m == 2:
                        dst = dst.rearrange("p (j d) -> p j d", j=FT)
                    sp.dma_start(dst, src).then_inc(ld_ew[m][e], 16)
                if e + 1 < NCH:
                    c = e + 1
                    sp.dma_start(x_sb[:, c * TILES:(c + 1) * TILES, :],
                                 x_dram[:, c * TILES:(c + 1) * TILES, :]).then_inc(ld_x[c], 16)
            for c in range(NCH):
                sp.wait_ge(y_done, c + 1)
                sp.dma_start(out_dram[:, c * TILES:(c + 1) * TILES, :], y[:]).then_inc(stored, 16)
            sp.wait_ge(stored, 16 * NCH)

        @block.gpsimd
        def _(pool):
            pool.dma_start(fwd_sb[:], fwd).then_inc(ld["fwd"], 16)
            pool.dma_start(inv_sb[:], inv).then_inc(ld["inv"], 16)
            nc.gpsimd.memset(minus_half[:], -0.5).then_inc(consts_set, 1)
            nc.gpsimd.memset(e_base[:], float(np.exp(1.0))).then_inc(consts_set, 1)
            nc.gpsimd.memset(ones_row[:], 1.0).then_inc(consts_set, 1)
            for s in range(3):
                nc.gpsimd.memset(up[s][:, :, 0:2], 0.0).then_inc(pads_set, 1)

            def inv_std(kind, c):
                pool.wait_ge(ln_mv[kind], TILES * (c + 1))
                nc.gpsimd.tensor_scalar(veps[kind][:], mv[kind][:, :, 1], EPS, None,
                                        ALU.add).then_inc(ln_veps[kind], 1)
                if kind in negm:
                    nc.gpsimd.tensor_scalar(negm[kind][:], mv[kind][:, :, 0], -1.0, None,
                                            ALU.mult).then_inc(ln_veps[kind], 1)
                pool.wait_ge(ln_veps[kind], (2 if kind in negm else 1) * (c + 1))
                if c == 0:
                    pool.wait_ge(consts_set, 3)
                nc.gpsimd.tensor_tensor(rstd[kind][:], veps[kind][:], minus_half[:],
                                        ALU.pow).then_inc(ln_rstd[kind], 1)
                if kind in negm:
                    pool.wait_ge(ln_rstd[kind], c + 1)
                    nc.gpsimd.tensor_tensor(nbias[kind][:], negm[kind][:], rstd[kind][:],
                                            ALU.mult).then_inc(ln_nbias[kind], 1)

            def split_expert(e):
                for m in range(3):
                    pool.wait_ge(ld_ew[m][e], 16)
                    raw = ew_sb[(3 * e + m) % EW_RING]
                    nc.gpsimd.tensor_scalar(ew_hi[m][:, e, :], raw[:], 1.0, None,
                                            ALU.mult).then_inc(ew_hi_done, 1)
                    pool.wait_ge(ew_hi_done, 3 * e + m + 1)
                    nc.gpsimd.tensor_tensor(ew_lo[m][:, e, :], raw[:],
                                            ew_hi[m][:, e, :].bitcast(F32),
                                            ALU.subtract).then_inc(ew_lo_done, 1)

            for g in range(FIRST, LAST):
                c, stage = hyena_at(g)
                if stage == 0:
                    inv_std("x", c)
                    if c == 0:
                        split_expert(0)
                        split_expert(1)
                if stage == 12:
                    inv_std("o", c)
                if stage == 13:
                    inv_std("x1", c)
                if 0 <= g < NG and g % STEPS == 0:
                    pool.wait_ge(lg_z_done, g // STEPS + 1)
                    nc.gpsimd.tensor_tensor(ge[:], e_base[:].rearrange("p (t e) -> p t e", e=NEXP),
                                            lg_z[:], ALU.pow).then_inc(ge_done, 1)
                if g == 0:
                    split_expert(2)
                    split_expert(3)
                if g >= STEPS and (g - 4) % STEPS == 0:
                    inv_std("moe", g // STEPS - 1)

        @block.tensor
        def _(pe):
            def product(dst, a_hi, a_lo, b_hi, b_lo, start=True, stop=True):
                nc.tensor.matmul(dst, a_hi, b_hi, start=start, stop=False)
                nc.tensor.matmul(dst, a_lo, b_hi, start=False, stop=False)
                return nc.tensor.matmul(dst, a_hi, b_lo, start=False, stop=stop)

            def transposes(dst, tile_of):
                for j in range(TILES):
                    last = nc.tensor.transpose(dst[:, j * P:(j + 1) * P], tile_of(j), ident_sb[:])
                return last

            def projection(c, s, bank):
                for n in range(3):
                    a = (w_in_hi, w_in_lo, w_in_hi)[n][:, s * P:(s + 1) * P]
                    b = (xnT_hi, xnT_hi, xnT_lo)[n][:]
                    if n == 2:
                        pe.wait_ge(xnT_lo_done, c + 1)
                    last = nc.tensor.matmul(bank[:], a, b, start=(n == 0), stop=(n == 2))
                last.then_inc(proj_mm[s], 1)

            def transform(c, half, bank):
                for i in range(2):
                    f0 = (2 * half + i) * P
                    for kt in range(2):
                        last = product(bank[:, i * BPC * P:(i + 1) * BPC * P],
                                       fwd_sb[:, 0, kt, f0:f0 + P], fwd_sb[:, 1, kt, f0:f0 + P],
                                       vT_hi[:, kt].rearrange("p b d -> p (b d)"),
                                       vT_lo[:, kt].rearrange("p b d -> p (b d)"),
                                       start=(kt == 0), stop=(kt == 1))
                last.then_inc(fwd_mm[half], 1)

            def filter_layer(n):
                bank = (ps_h1[0], ps_h1[1], ps_h3[0])[n]
                if n == 0:
                    pe.wait_ge(ld["fz"], 16)
                    last = nc.tensor.matmul(bank[:, 0:SEQ], filt_z_sb[:, 0:P], filt_z_sb[:, P:P + SEQ],
                                            start=True, stop=True)
                else:
                    if n == 1:
                        pe.wait_ge(ld["fmats"], 16)
                    pe.wait_ge(f_sin, n)
                    last = nc.tensor.matmul(bank[:, 0:SEQ], filt_mats_sb[:, n - 1, :], fh,
                                            start=True, stop=True)
                last.then_inc(f_mm, 1)

            def filter_taps():
                pe.wait_ge(f_sin, 3)
                half = P // 2
                for i in range(4):
                    h = i // 2
                    bank = (ps_h3[1], ps_et)[h]
                    last = nc.tensor.matmul(bank[:, (i % 2) * P:(i % 2 + 1) * P],
                                            fh[h * half:(h + 1) * half, (i % 2) * P:(i % 2 + 1) * P],
                                            filt_mats_sb[h * half:(h + 1) * half, 2, :],
                                            start=True, stop=True)
                    if i % 2:
                        last.then_inc(taps_mm, 1)

            def filter_transform():
                pe.wait_ge(ld["fwd"], 16)
                pe.wait_ge(fold_hi_done, 1)
                pe.wait_ge(fold_lo_done, 1)
                for i in range(4):
                    for kt in range(2):
                        last = product(ps_eo[:, i * P:(i + 1) * P],
                                       fwd_sb[:, 0, kt, i * P:(i + 1) * P],
                                       fwd_sb[:, 1, kt, i * P:(i + 1) * P],
                                       fold_hi[:, i // 2, kt * P:(kt + 1) * P],
                                       fold_lo[:, i // 2, kt * P:(kt + 1) * P],
                                       start=(kt == 0), stop=(kt == 1))
                last.then_inc(khat_mm, 1)

            def hyena(c, stage):
                if stage == 1:
                    if c == 0:
                        filter_layer(0)
                        pe.wait_ge(ld["ident"], 16)
                    pe.wait_ge(xn_done, TILES * (c + 1))
                    if c > 0:
                        pe.wait_ge(lg_done, c)
                    transposes(ps_a, lambda j: xn[:, j, :]).then_inc(xnT_mm, 1)
                if stage == 2:
                    if c == 0:
                        pe.wait_ge(w_in_hi_done, 1)
                        pe.wait_ge(w_in_lo_done, 1)
                        filter_layer(1)
                    pe.wait_ge(xnT_hi_done, c + 1)
                    if c > 0:
                        pe.wait_ge(xfT_lo_done, c)
                    projection(c, X1, ps_b)
                if stage == 3:
                    projection(c, V, ps_a)
                if stage == 4:
                    pe.wait_ge(up_done[X1], c + 1)
                    pe.wait_ge(tap2_done[X1], c + 1)
                    projection(c, X0, ps_b)
                    if c == 0:
                        filter_layer(2)
                if stage == 5:
                    pe.wait_ge(up_done[V], c + 1)
                    pe.wait_ge(tap2_done[V], c + 1)
                    pe.wait_ge(vx_done, c + 1)
                    for kt in range(2):
                        for b in range(BPC):
                            at = (kt * BPC + b) * P
                            last = nc.tensor.transpose(ps_a[:, at:at + P], vx[:, b, kt * P:(kt + 1) * P],
                                                       ident_sb[:])
                    last.then_inc(vT_mm, 1)
                    if c == 0:
                        filter_taps()
                if stage == 6:
                    if c == 0:
                        pe.wait_ge(ld["fwd"], 16)
                    pe.wait_ge(up_done[X0], c + 1)
                    pe.wait_ge(tap2_done[X0], c + 1)
                    pe.wait_ge(vT_hi_done, c + 1)
                    pe.wait_ge(vT_lo_done, c + 1)
                    transform(c, 0, ps_b)
                if stage == 7:
                    transform(c, 1, ps_a)
                    if c == 0:
                        filter_transform()
                if stage == 10:
                    if c == 0:
                        pe.wait_ge(ld["inv"], 16)
                    for h in range(2):
                        pe.wait_ge(yh_hi_done[h], c + 1)
                        pe.wait_ge(yh_lo_done[h], c + 1)
                    for b in range(BPC):
                        for i in range(4):
                            hi = yh_hi[:, i // 2, i % 2, b * P:(b + 1) * P]
                            lo = yh_lo[:, i // 2, i % 2, b * P:(b + 1) * P]
                            last = product(ps_b[:, b * SEQ:(b + 1) * SEQ], hi, lo,
                                           inv_sb[:, 0, i, :], inv_sb[:, 1, i, :],
                                           start=(i == 0), stop=(i == 3))
                    last.then_inc(y_mm, 1)
                if stage == 11:
                    if c == 0:
                        pe.wait_ge(w_out_hi_done, 1)
                        pe.wait_ge(w_out_lo_done, 3)
                    pe.wait_ge(gated_hi_done, c + 1)
                    pe.wait_ge(gated_lo_done, c + 1)
                    nc.tensor.matmul(ps_a[:], ones_r[:], rows_hi[:], start=True, stop=False,
                                     skip_group_check=True)
                    nc.tensor.matmul(ps_a[:], ones_r[:], rows_lo[:], start=False, stop=False,
                                     skip_group_check=True)
                    for j in range(TILES):
                        t = slice(j * P, (j + 1) * P)
                        for n in range(3):
                            last = nc.tensor.matmul(ps_a[:, t], (gated_hi, gated_lo, gated_hi)[n][:, t],
                                                    (w_out_hi, w_out_hi, w_out_lo)[n][:],
                                                    start=False, stop=(n == 2), skip_group_check=True)
                    last.then_inc(o_mm, 1)
                if stage == 15:
                    pe.wait_ge(xf_done, TILES * (c + 1))
                    transposes(ps_b, lambda j: xf[:, j, :]).then_inc(xfT_mm, 1)

            def logits(c):
                if c == 0:
                    pe.wait_ge(router_hi_done, 1)
                    pe.wait_ge(router_lo_done, 1)
                for j in range(TILES):
                    t = slice(j * P, (j + 1) * P)
                    dst = ps_a[:, j * 2 * NEXP:(j + 1) * 2 * NEXP]
                    nc.tensor.matmul(dst, xfT_hi[:, c % 2, t], router_hl[:], start=True, stop=False)
                    last = nc.tensor.matmul(dst, xfT_lo[:, c % 2, t], router_hl[:], start=False, stop=True)
                last.then_inc(logits_mm, 1)

            def up_products(g):
                c, k = divmod(g, STEPS)
                e, f = divmod(k, FT)
                if k == 0:
                    pe.wait_ge(xfT_hi_done, c + 1)
                    pe.wait_ge(xfT_lo_done, c + 1)
                if c == 0 and f == 0:
                    pe.wait_ge(ew_lo_done, 3 * e + 2)
                fs = slice(f * P, (f + 1) * P)
                if g >= 2:
                    pe.wait_ge(silu_done, g - 1)
                product(ps_h1[g % 2][:], ew_hi[0][:, e, fs], ew_lo[0][:, e, fs],
                        xfT_hi[:, c % 2], xfT_lo[:, c % 2]).then_inc(h1_mm, 1)
                if g >= 2:
                    pe.wait_ge(hid_done, g - 1)
                product(ps_h3[g % 2][:], ew_hi[1][:, e, fs], ew_lo[1][:, e, fs],
                        xfT_hi[:, c % 2], xfT_lo[:, c % 2]).then_inc(h3_mm, 1)

            def down_product(g):
                c, k = divmod(g, STEPS)
                e, f = divmod(k, FT)
                if c == 0 and f == 0:
                    pe.wait_ge(ew_lo_done, 3 * e + 3)
                if f == 0 and g > 0:
                    pe.wait_ge(eoT_done, g // FT)
                pe.wait_ge(hid_hi_done, g + 1)
                pe.wait_ge(hid_lo_done, g + 1)
                fs = slice(f * P, (f + 1) * P)
                product(ps_eo[:], ew_hi[2][:, e, fs], ew_lo[2][:, e, fs], hid_hi[:, g % 4], hid_lo[:, g % 4],
                        start=(f == 0), stop=(f == FT - 1)).then_inc(eo_mm, 1)

            for g in range(FIRST, LAST):
                c, stage = hyena_at(g)
                if 0 <= g < NG:
                    up_products(g)
                if 0 <= g - 2 < NG:
                    down_product(g - 2)
                if g >= 6 and (g - 6) % FT == 0 and (g - 6) // FT < NG // FT:
                    n = (g - 6) // FT
                    pe.wait_ge(eoT_done, n + 1)
                    if n > 0:
                        pe.wait_ge(acc_done, TILES * n)
                    transposes(ps_et, lambda j: eoT[:, j * P:(j + 1) * P]).then_inc(et_mm, 1)
                if 0 <= g < NG and g % STEPS == 0:
                    logits(g // STEPS)
                if stage is not None:
                    hyena(c, stage)

        @block.scalar
        def _(act):
            act.dma_start(cols_sb[:], cols).then_inc(ld["cols"], 16)
            act.dma_start(ident_sb[:], ident).then_inc(ld["ident"], 16)
            act.dma_start(w_in_sb[:], w_in).then_inc(ld["w_in"], 16)
            act.dma_start(rows_sb[:], rows).then_inc(ld["rows"], 16)
            act.dma_start(w_out_sb[:], w_out).then_inc(ld["w_out"], 16)
            act.dma_start(router_sb[:], router).then_inc(ld["router"], 16)
            act.dma_start(tri_sb[:], tri).then_inc(ld["tri"], 16)

            def filter_sin(n):
                act.wait_ge(f_red, n + 1)
                nc.scalar.activation(fh, fred, ACT.Sin).then_inc(f_sin, 1)

            def khat_tables():
                act.wait_ge(khat_mm, 1)
                kh = ps_eo[:].rearrange("p (i d) -> p i d", i=4)

                def both(i):
                    return kh[:, i:i + 1, :].broadcast_to([P, BPC, P])
                for i in range(4):
                    nc.scalar.activation(khat_a[:, i], both(i - i % 2), ACT.Copy).then_inc(khat_copied, 1)
                for i in range(4):
                    nc.scalar.activation(khat_b[:, i], both(i - i % 2 + 1), ACT.Copy,
                                         scale=(1.0 if i % 2 else -1.0)).then_inc(khat_copied, 1)
                act.wait_ge(khat_copied, 8)
                nc.scalar.activation(khat_a[0:1, 1], both(1)[0:1], ACT.Copy).then_inc(khat_copied, 1)

            def up_and_tap2(c, s, bank):
                act.wait_ge(proj_mm[s], c + 1)
                src = bank[:].rearrange("p (b t) -> p b t", b=BPC)
                if c > 0:
                    act.wait_ge(uc_done[s], c)
                nc.scalar.activation(up[s][:, :, 2:], src, ACT.Identity,
                                     bias=cols_sb[:, C_BIN + s:C_BIN + s + 1]).then_inc(up_done[s], 1)
                nc.scalar.activation(tap2[s][:], src, ACT.Identity,
                                     scale=cols_sb[:, C_SFW + 3 * s + 2:C_SFW + 3 * s + 3],
                                     bias=tap2_bias[:, s:s + 1]).then_inc(tap2_done[s], 1)

            def normed(kind, c, dst, src, done):
                act.wait_ge(ln_nbias[kind], c + 1)
                for j in range(TILES):
                    nc.scalar.activation(dst[:, j, :], src(j), ACT.Identity, bias=nbias[kind][:, j:j + 1],
                                         scale=rstd[kind][:, j:j + 1]).then_inc(done, 1)

            def hyena(c, stage):
                if stage == 0 and c == 0:
                    act.wait_ge(ld["w_in"], 16)
                    nc.scalar.activation(w_in_hi[:], w_in_sb[:], ACT.Copy).then_inc(w_in_hi_done, 1)
                if stage == 1:
                    act.wait_ge(xnT_mm, c + 1)
                    nc.scalar.activation(xnT_hi[:], ps_a[:], ACT.Copy).then_inc(xnT_hi_done, 1)
                    if c == 0:
                        filter_sin(0)
                        act.wait_ge(tap2_bias_done, 1)
                        act.wait_ge(pads_set, 3)
                if stage == 2:
                    up_and_tap2(c, X1, ps_b)
                    if c == 0:
                        filter_sin(1)
                if stage == 3:
                    up_and_tap2(c, V, ps_a)
                if stage == 4:
                    if c == 0:
                        filter_sin(2)
                    up_and_tap2(c, X0, ps_b)
                if stage == 5:
                    act.wait_ge(vT_mm, c + 1)
                    nc.scalar.activation(vT_hi[:].rearrange("p k b d -> p (k b d)"), ps_a[:],
                                         ACT.Copy).then_inc(vT_hi_done, 1)
                    if c == 0:
                        act.wait_ge(fold_done, 2)
                        nc.scalar.activation(fold_hi, fold, ACT.Copy).then_inc(fold_hi_done, 1)
                if stage == 7 and c == 0:
                    khat_tables()
                    act.wait_ge(ld["rows"], 16)
                    nc.scalar.activation(rows_hi[:], rows_sb[:, 0:4 * P], ACT.Copy).then_inc(w_out_hi_done, 1)
                    act.wait_ge(consts_set, 3)
                    nc.scalar.activation(ones_r[:], ones_row[:], ACT.Copy).then_inc(w_out_hi_done, 1)
                    act.wait_ge(ld["w_out"], 16)
                    nc.scalar.activation(w_out_hi[:], w_out_sb[:], ACT.Copy).then_inc(w_out_hi_done, 1)
                    act.wait_ge(ld["router"], 16)
                    nc.scalar.activation(router_hl[:, 0:NEXP], router_sb[:], ACT.Copy).then_inc(router_hi_done, 1)
                if stage in (8, 9):
                    h = stage - 8
                    act.wait_ge(yh_done[h], c + 1)
                    nc.scalar.activation(yh_hi[:, h], yh[:, h], ACT.Copy).then_inc(yh_hi_done[h], 1)
                if stage == 11:
                    act.wait_ge(gated_done, c + 1)
                    nc.scalar.activation(gated_hi[:], gated[:], ACT.Copy).then_inc(gated_hi_done, 1)
                if stage == 13:
                    normed("o", c, o_n, lambda j: ps_a[:, j * P:(j + 1) * P], o_n_done)
                if stage == 15:
                    act.wait_ge(xfT_mm, c + 1)
                    nc.scalar.activation(xfT_hi[:, c % 2], ps_b[:], ACT.Copy).then_inc(xfT_hi_done, 1)

            for g in range(FIRST, LAST):
                c, stage = hyena_at(g)
                if 0 <= g < NG:
                    act.wait_ge(h1_mm, g + 1)
                    if g >= 2:
                        act.wait_ge(hid_done, g - 1)
                    nc.scalar.activation(silu[:, g % 2], ps_h1[g % 2][:], ACT.Silu).then_inc(silu_done, 1)
                if 0 <= g - 1 < NG:
                    act.wait_ge(hid_done, g)
                    nc.scalar.activation(hid_hi[:, (g - 1) % 4], hid[:, (g - 1) % 2],
                                         ACT.Copy).then_inc(hid_hi_done, 1)
                if g >= 5 and (g - 5) % FT == 0 and (g - 5) // FT < NG // FT:
                    n = (g - 5) // FT
                    act.wait_ge(eo_mm, FT * (n + 1))
                    if n > 0:
                        act.wait_ge(et_mm, n)
                    nc.scalar.activation(eoT[:], ps_eo[:], ACT.Copy).then_inc(eoT_done, 1)
                if g >= STEPS and (g - 5) % STEPS == 0:
                    if g // STEPS >= 2:
                        act.wait_ge(stored, 16 * (g // STEPS - 1))
                    normed("moe", g // STEPS - 1, acc_n, lambda j: acc[:, j, :], acc_n_done)
                if stage is not None:
                    hyena(c, stage)

        @block.vector
        def _(dve):
            def moments(kind, c, src):
                for j in range(TILES):
                    nc.vector.bn_stats(stats[kind][:, j, :], src(j)).then_inc(ln_stats[kind], 1)
                for j in range(TILES):
                    dve.wait_ge(ln_stats[kind], TILES * c + j + 1)
                    nc.vector.bn_aggr(mv[kind][:, j, :], stats[kind][:, j, :]).then_inc(ln_mv[kind], 1)

            def normalise(kind, c, dst, src, done):
                dve.wait_ge(ln_rstd[kind], c + 1)
                for j in range(TILES):
                    nc.vector.tensor_scalar(dst[:, j, :], src(j), mv[kind][:, j, 0:1], rstd[kind][:, j:j + 1],
                                            ALU.subtract, ALU.mult).then_inc(done, 1)

            def filter_reduce(n):
                bank = (ps_h1[0], ps_h1[1], ps_h3[0])[n]
                dve.wait_ge(f_mm, n + 1)
                nc.vector.tensor_scalar(farg, bank[:, 0:SEQ], cols_sb[:, C_FB + n:C_FB + n + 1],
                                        cols_sb[:, C_FF + n:C_FF + n + 1], ALU.add, ALU.mult).then_inc(f_step, 1)
                dve.wait_ge(f_step, 5 * n + 1)
                nc.vector.tensor_scalar(fturn, farg, 1.0 / TWO_PI, ROUND, ALU.mult, ALU.add).then_inc(f_step, 1)
                dve.wait_ge(f_step, 5 * n + 2)
                nc.vector.tensor_scalar(fturn, fturn, ROUND, None, ALU.subtract).then_inc(f_step, 1)
                dve.wait_ge(f_step, 5 * n + 3)
                nc.vector.scalar_tensor_tensor(out=farg, in0=fturn, scalar=-TWO_PI_HI, in1=farg,
                                               op0=ALU.mult, op1=ALU.add).then_inc(f_step, 1)
                dve.wait_ge(f_step, 5 * n + 4)
                nc.vector.scalar_tensor_tensor(out=farg, in0=fturn, scalar=-(TWO_PI - TWO_PI_HI), in1=farg,
                                               op0=ALU.mult, op1=ALU.add).then_inc(f_step, 1)
                dve.wait_ge(f_step, 5 * n + 5)
                nc.vector.tensor_scalar(fred, farg, -PI_BELOW, PI_BELOW, ALU.max, ALU.min).then_inc(f_red, 1)

            def filter_fold():
                dve.wait_ge(taps_mm, 2)
                dve.wait_ge(ld["decay"], 16)
                for h, bank in enumerate((ps_h3[1], ps_et)):
                    nc.vector.tensor_tensor(taps[:, 2 * h:2 * h + 2].rearrange("p i d -> p (i d)"), bank[:, 0:2 * P],
                                            decay_sb[:, 2 * h:2 * h + 2].rearrange("p i d -> p (i d)"),
                                            ALU.mult).then_inc(taps_done, 1)
                dve.wait_ge(taps_done, 2)
                dve.wait_ge(ld["rows"], 16)
                nc.vector.tensor_tensor(taps[0:1, 0, :], taps[0:1, 0, :], rows_sb[:, 4 * P:5 * P],
                                        ALU.add).then_inc(taps_done, 1)
                dve.wait_ge(taps_done, 3)
                for h, op in enumerate((ALU.add, ALU.subtract)):
                    nc.vector.tensor_tensor(fold[:, h], taps[:, 0:2].rearrange("p i d -> p (i d)"),
                                            taps[:, 2:4].rearrange("p i d -> p (i d)"), op).then_inc(fold_done, 1)
                dve.wait_ge(fold_hi_done, 1)
                nc.vector.tensor_tensor(fold_lo, fold, fold_hi.bitcast(F32),
                                        ALU.subtract).then_inc(fold_lo_done, 1)

            def short_conv(c, s):
                src = up[s]
                dve.wait_ge(up_done[s], c + 1)
                dve.wait_ge(tap2_done[s], c + 1)
                nc.vector.scalar_tensor_tensor(out=uc[s][:], in0=src[:, :, 1:SEQ + 1],
                                               scalar=cols_sb[:, C_SFW + 3 * s + 1:C_SFW + 3 * s + 2],
                                               in1=tap2[s][:], op0=ALU.mult, op1=ALU.add).then_inc(tap1_done[s], 1)
                dve.wait_ge(tap1_done[s], c + 1)
                nc.vector.scalar_tensor_tensor(out=uc[s][:], in0=src[:, :, 0:SEQ],
                                               scalar=cols_sb[:, C_SFW + 3 * s:C_SFW + 3 * s + 1],
                                               in1=uc[s][:], op0=ALU.mult, op1=ALU.add).then_inc(uc_done[s], 1)

            def spectrum_product(c, h, bank):
                dve.wait_ge(fwd_mm[h], c + 1)
                src = bank[:].rearrange("p (i n) -> p i n", i=2)
                ka = khat_a[:, 2 * h:2 * h + 2].rearrange("p i b d -> p i (b d)")
                kb = khat_b[:, 2 * h:2 * h + 2].rearrange("p i b d -> p i (b d)")
                nc.vector.tensor_tensor(pa[:, h], src, ka, ALU.mult).then_inc(prod_a[h], 1)
                nc.vector.tensor_tensor(pb[:, h], src[:, ::-1], kb, ALU.mult).then_inc(prod_b[h], 1)
                dve.wait_ge(prod_a[h], c + 1)
                dve.wait_ge(prod_b[h], c + 1)
                nc.vector.tensor_tensor(yh[:, h], pa[:, h], pb[:, h], ALU.add).then_inc(yh_done[h], 1)

            def hyena(c, stage):
                if stage == 0:
                    dve.wait_ge(ld_x[c], 16)
                    moments("x", c, lambda j: x_sb[:, c * TILES + j, :])
                    if c == 0:
                        dve.wait_ge(w_in_hi_done, 1)
                        nc.vector.tensor_tensor(w_in_lo[:], w_in_sb[:], w_in_hi[:].bitcast(F32),
                                                ALU.subtract).then_inc(w_in_lo_done, 1)
                    normalise("x", c, xn, lambda j: x_sb[:, c * TILES + j, :], xn_done)
                    if c == 0:
                        dve.wait_ge(ld["cols"], 16)
                        tap_w2 = cols_sb[:, C_SFW:C_SFW + 9].rearrange("p (s k) -> p s k", k=3)[:, :, 2]
                        nc.vector.tensor_tensor(tap2_bias[:], tap_w2, cols_sb[:, C_BIN:C_BIN + 3],
                                                ALU.mult).then_inc(tap2_bias_a, 1)
                        dve.wait_ge(tap2_bias_a, 1)
                        nc.vector.tensor_tensor(tap2_bias[:], tap2_bias[:], cols_sb[:, C_SFB:C_SFB + 3],
                                                ALU.add).then_inc(tap2_bias_done, 1)
                        filter_reduce(0)
                if stage == 1:
                    dve.wait_ge(xnT_hi_done, c + 1)
                    nc.vector.tensor_tensor(xnT_lo[:], ps_a[:], xnT_hi[:].bitcast(F32),
                                            ALU.subtract).then_inc(xnT_lo_done, 1)
                    if c == 0:
                        filter_reduce(1)
                if stage == 3:
                    short_conv(c, X1)
                if stage == 4:
                    short_conv(c, V)
                    dve.wait_ge(uc_done[V], c + 1)
                    nc.vector.tensor_tensor(vx[:], uc[V][:], uc[X1][:], ALU.mult).then_inc(vx_done, 1)
                    if c == 0:
                        filter_reduce(2)
                if stage == 5:
                    dve.wait_ge(vT_hi_done, c + 1)
                    nc.vector.tensor_tensor(vT_lo[:].rearrange("p k b d -> p (k b d)"), ps_a[:],
                                            vT_hi[:].rearrange("p k b d -> p (k b d)").bitcast(F32),
                                            ALU.subtract).then_inc(vT_lo_done, 1)
                    if c == 0:
                        filter_fold()
                if stage == 6:
                    short_conv(c, X0)
                if stage == 7:
                    if c == 0:
                        dve.wait_ge(khat_copied, 9)
                        nc.vector.memset(khat_b[0:1, 0:2], 0.0).then_inc(khat_zeroed, 1)
                        dve.wait_ge(khat_zeroed, 1)
                    spectrum_product(c, 0, ps_b)
                if stage == 8:
                    spectrum_product(c, 1, ps_a)
                    if c == 0:
                        dve.wait_ge(w_out_hi_done, 3)
                        nc.vector.tensor_tensor(rows_lo[:], rows_sb[:, 0:4 * P], rows_hi[:].bitcast(F32),
                                                ALU.subtract).then_inc(w_out_lo_done, 1)
                        nc.vector.tensor_tensor(w_out_lo[:], w_out_sb[:], w_out_hi[:].bitcast(F32),
                                                ALU.subtract).then_inc(w_out_lo_done, 2)
                        dve.wait_ge(router_hi_done, 1)
                        nc.vector.tensor_tensor(router_hl[:, NEXP:2 * NEXP], router_sb[:],
                                                router_hl[:, 0:NEXP].bitcast(F32),
                                                ALU.subtract).then_inc(router_lo_done, 1)
                if stage in (8, 9):
                    h = stage - 8
                    dve.wait_ge(yh_hi_done[h], c + 1)
                    nc.vector.tensor_tensor(yh_lo[:, h], yh[:, h], yh_hi[:, h].bitcast(F32),
                                            ALU.subtract).then_inc(yh_lo_done[h], 1)
                if stage == 11:
                    dve.wait_ge(y_mm, c + 1)
                    dve.wait_ge(uc_done[X0], c + 1)
                    nc.vector.tensor_tensor(gated[:], ps_b[:], uc[X0][:].rearrange("p b t -> p (b t)"),
                                            ALU.mult).then_inc(gated_done, 1)
                    dve.wait_ge(gated_hi_done, c + 1)
                    nc.vector.tensor_tensor(gated_lo[:], gated[:], gated_hi[:].bitcast(F32),
                                            ALU.subtract).then_inc(gated_lo_done, 1)
                if stage == 12:
                    dve.wait_ge(o_mm, c + 1)
                    moments("o", c, lambda j: ps_a[:, j * P:(j + 1) * P])
                if stage == 13:
                    dve.wait_ge(o_n_done, TILES * (c + 1))
                    nc.vector.tensor_tensor(x1[:, c % 2], o_n[:], x_sb[:, c * TILES:(c + 1) * TILES, :],
                                            ALU.add).then_inc(x1_done, 1)
                    dve.wait_ge(x1_done, c + 1)
                    moments("x1", c, lambda j: x1[:, c % 2, j, :])
                if stage == 14:
                    normalise("x1", c, xf, lambda j: x1[:, c % 2, j, :], xf_done)
                if stage == 15:
                    dve.wait_ge(xfT_hi_done, c + 1)
                    nc.vector.tensor_tensor(xfT_lo[:, c % 2], ps_b[:], xfT_hi[:, c % 2].bitcast(F32),
                                            ALU.subtract).then_inc(xfT_lo_done, 1)

            def gates_a(c):
                dve.wait_ge(logits_mm, c + 1)
                src = ps_a[:, 0:TILES * 2 * NEXP].rearrange("p (t h e) -> p t h e", t=TILES, h=2)
                rb = cols_sb[:, C_RB:C_RB + NEXP].unsqueeze(1).broadcast_to([P, TILES, NEXP])
                nc.vector.tensor_tensor(lg_a[:], src[:, :, 0, :], rb, ALU.add).then_inc(lg_a_done, 1)
                dve.wait_ge(lg_a_done, c + 1)
                nc.vector.tensor_tensor(lg[:], src[:, :, 1, :], lg_a[:], ALU.add).then_inc(lg_done, 1)
                dve.wait_ge(lg_done, c + 1)
                nc.vector.reduce_max(lg_max[:], lg[:], AX_X).then_inc(lg_max_done, 1)
                dve.wait_ge(lg_max_done, c + 1)
                nc.vector.tensor_tensor(lg_z[:], lg[:], lg_max[:].unsqueeze(2).broadcast_to([P, TILES, NEXP]),
                                        ALU.subtract).then_inc(lg_z_done, 1)

            def gates_b(c):
                full = [P, TILES, NEXP, NEXP]
                dve.wait_ge(ge_done, c + 1)
                other = ge[:].unsqueeze(2).broadcast_to(full)
                own = ge[:].unsqueeze(3).broadcast_to(full)
                flat = "p t i j -> p t (i j)"
                nc.vector.tensor_tensor(beats[:], other, own, ALU.is_gt).then_inc(beats_done, 1)
                nc.vector.tensor_tensor(ties[:], other, own, ALU.is_equal).then_inc(ties_done, 1)
                dve.wait_ge(ties_done, c + 1)
                if c == 0:
                    dve.wait_ge(ld["tri"], 16)
                nc.vector.tensor_tensor(ties_low[:].rearrange(flat), ties[:].rearrange(flat),
                                        tri_sb[:].unsqueeze(1).broadcast_to([P, TILES, NEXP * NEXP]),
                                        ALU.mult).then_inc(ties_low_done, 1)
                dve.wait_ge(beats_done, c + 1)
                dve.wait_ge(ties_low_done, c + 1)
                nc.vector.tensor_tensor(ahead[:], beats[:], ties_low[:], ALU.add).then_inc(ahead_done, 1)
                dve.wait_ge(ahead_done, c + 1)
                nc.vector.reduce_sum(place[:], ahead[:], AX_X).then_inc(place_done, 1)
                dve.wait_ge(place_done, c + 1)
                nc.vector.scalar_tensor_tensor(out=kept[:], in0=place[:], scalar=2.0, in1=ge[:],
                                               op0=ALU.is_lt, op1=ALU.mult).then_inc(kept_done, 1)
                dve.wait_ge(kept_done, c + 1)
                nc.vector.reduce_sum(ksum[:], kept[:], AX_X).then_inc(ksum_done, 1)
                dve.wait_ge(ksum_done, c + 1)
                nc.vector.reciprocal(krec[:], ksum[:]).then_inc(krec_done, 1)
                dve.wait_ge(krec_done, c + 1)
                nc.vector.tensor_tensor(gates[:, c % 2], kept[:],
                                        krec[:].unsqueeze(2).broadcast_to([P, TILES, NEXP]),
                                        ALU.mult).then_inc(gates_done, 1)

            def add_expert(n):
                c, e = divmod(n, NEXP)
                dve.wait_ge(et_mm, n + 1)
                if e == 0:
                    dve.wait_ge(gates_done, c + 1)
                    if c > 0:
                        dve.wait_ge(acc_n_done, TILES * c)
                else:
                    dve.wait_ge(acc_done, TILES * n)
                for j in range(TILES):
                    src, gate = ps_et[:, j * P:(j + 1) * P], gates[:, c % 2, j, e:e + 1]
                    if e == 0:
                        nc.vector.tensor_scalar(acc[:, j, :], src, gate, None, ALU.mult).then_inc(acc_done, 1)
                    else:
                        nc.vector.scalar_tensor_tensor(out=acc[:, j, :], in0=src, scalar=gate, in1=acc[:, j, :],
                                                       op0=ALU.mult, op1=ALU.add).then_inc(acc_done, 1)

            for g in range(FIRST, LAST):
                c, stage = hyena_at(g)
                if 0 <= g < NG:
                    dve.wait_ge(silu_done, g + 1)
                    dve.wait_ge(h3_mm, g + 1)
                    if g >= 2:
                        dve.wait_ge(hid_hi_done, g - 1)
                        dve.wait_ge(hid_lo_done, g - 1)
                    nc.vector.tensor_tensor(hid[:, g % 2], ps_h3[g % 2][:], silu[:, g % 2],
                                            ALU.mult).then_inc(hid_done, 1)
                if 0 <= g - 1 < NG:
                    dve.wait_ge(hid_hi_done, g)
                    nc.vector.tensor_tensor(hid_lo[:, (g - 1) % 4], hid[:, (g - 1) % 2],
                                            hid_hi[:, (g - 1) % 4].bitcast(F32),
                                            ALU.subtract).then_inc(hid_lo_done, 1)
                if g >= 7 and (g - 7) % FT == 0 and (g - 7) // FT < NG // FT:
                    add_expert((g - 7) // FT)
                if 0 <= g < NG and g % STEPS == 0:
                    gates_a(g // STEPS)
                if 0 <= g < NG and g % STEPS == 2:
                    gates_b(g // STEPS)
                if g >= STEPS and (g - 4) % STEPS == 0:
                    cc = g // STEPS - 1
                    dve.wait_ge(acc_done, TILES * NEXP * (cc + 1))
                    moments("moe", cc, lambda j: acc[:, j, :])
                if g >= STEPS and (g - 5) % STEPS == 0:
                    cc = g // STEPS - 1
                    dve.wait_ge(acc_n_done, TILES * (cc + 1))
                    nc.vector.tensor_tensor(y[:], acc_n[:], x1[:, cc % 2], ALU.add).then_inc(y_done, 1)
                if stage is not None:
                    hyena(c, stage)


def _split_table(t):
    t = t.astype(np.float32)
    bits = t.view(np.uint32).astype(np.uint64)
    bits = ((bits + 0x7FF + ((bits >> 12) & 1)) & 0xFFFFF000).astype(np.uint32)
    hi = bits.view(np.float32)
    return hi, t - hi


def _transform_tables():
    n = LFILT
    t = np.arange(SEQ, dtype=np.int64)
    even, odd = 2 * np.arange(P), 2 * np.arange(P) + 1

    def turn(f):
        return 2 * np.pi * ((t[:, None] * f[None, :]) % n) / n

    alternate = np.where(t % 2 == 0, 1.0, -1.0)
    forward = [np.cos(turn(even)), -np.sin(turn(even)), np.cos(turn(odd)), -np.sin(turn(odd))]
    forward[1][:, 0] = alternate
    inverse = [2 / n * np.cos(turn(even)).T, -2 / n * np.sin(turn(even)).T,
               2 / n * np.cos(turn(odd)).T, -2 / n * np.sin(turn(odd)).T]
    inverse[0][0] = 1 / n
    inverse[1][0] = alternate / n
    fwd = np.stack(_split_table(np.concatenate(forward, 1).reshape(2, P, LFILT)))
    inv = np.stack(_split_table(np.stack(inverse)))
    return (np.ascontiguousarray(fwd.transpose(2, 0, 1, 3)), np.ascontiguousarray(inv.transpose(2, 0, 1, 3)))


def _filter_tables():
    t = np.linspace(0.0, 1.0, LFILT).astype(np.float32)
    w = (2.0 * np.pi * np.arange(LFILT) / LFILT).astype(np.float32)
    fw = (np.float32(1e-4) * w).astype(np.float64)
    z = np.stack([t, np.cos(fw), -np.sin(fw)]).astype(np.float32)
    deltas = np.linspace(np.log(0.01) / 1.5, np.log(0.01) / 0.3, P)
    window = np.exp(-t[:, None].astype(np.float64) * np.abs(deltas)[None, :]) + 0.05
    return z, window.astype(np.float32)


def kernel(**inputs):
    import concourse.bacc as _bacc
    from concourse.bass_utils import run_bass_kernel_spmd as _run

    d = {k.removeprefix("L0_"): np.asarray(v) for k, v in inputs.items()}
    u = d["attn_u"]
    x = np.ascontiguousarray(u.reshape(-1, P))
    z, window = _filter_tables()
    fwd, inv = _transform_tables()
    half = P // 2

    def twice(v):
        return np.concatenate([v, v])[:, None]

    cols = np.concatenate(
        [d["attn_b_in"].reshape(3, P).T,
         d["attn_sf_w"].reshape(3, P, 3).transpose(1, 0, 2).reshape(P, 9),
         d["attn_sf_b"].reshape(3, P).T,
         *(twice(d[f"attn_f_b{n}"]) for n in (1, 2, 3)),
         *(twice(d[f"attn_freq{n}"]) for n in (1, 2, 3)),
         np.broadcast_to(d["ffn_router_b"], (P, NEXP))], axis=1)
    rows = np.concatenate([d["attn_b_out"]] * 4 + [d["attn_filt_bias"]])[None, :]
    filt_z = np.zeros((6, P + SEQ), np.float32)
    filt_mats = np.zeros((P, 3, P), np.float32)
    for h in range(2):
        a = slice(h * half, (h + 1) * half)
        filt_z[3 * h:3 * h + 3, a] = d["attn_f_w1"]
        filt_z[3 * h:3 * h + 3, P:] = z[:, h * SEQ:(h + 1) * SEQ]
        filt_mats[a, 0, a] = d["attn_f_w2"]
        filt_mats[a, 1, a] = d["attn_f_w3"]
        filt_mats[a, 2, :] = d["attn_f_wout"]
    arrays = {
        "x": x, "w_in": d["attn_w_in"], "w_out": d["attn_w_out"], "cols": cols, "rows": rows,
        "filt_z": filt_z, "filt_mats": filt_mats,
        "decay": np.ascontiguousarray(window.reshape(4, P, P).transpose(1, 0, 2)),
        "router": d["ffn_router_w"], "w1": d["ffn_w1"], "w3": d["ffn_w3"], "w2": d["ffn_w2"],
        "fwd": fwd, "inv": inv, "ident": np.eye(P, dtype=np.float32),
        "tri": np.ascontiguousarray(np.broadcast_to(np.tril(np.ones((NEXP, NEXP), np.float32), -1).reshape(1, -1),
                                                    (P, NEXP * NEXP))),
    }
    nc = _bacc.Bacc("TRN2", target_bir_lowering=False, num_devices=1)
    ins, args = {}, {}
    for name, a in arrays.items():
        a = np.ascontiguousarray(a)
        ins[f"in_{name}"] = a
        args[name] = nc.dram_tensor(f"in_{name}", a.shape, mybir.dt.from_np(a.dtype), kind="ExternalInput").ap()
    out = nc.dram_tensor("out_x", x.shape, F32, kind="ExternalOutput").ap()
    build(nc, out=out, **args)
    got = _run(nc, [ins], core_ids=[0]).results[0]["out_x"]
    return got.reshape(u.shape)
```

```python
from contextlib import ExitStack

import numpy as np

import concourse.bass as bass
from concourse import mybir

F32 = mybir.dt.float32
F32R = mybir.dt.float32r
ALU = mybir.AluOpType
ACT = mybir.ActivationFunctionType
AX_X = mybir.AxisListType.X

P = 128
LFILT = 512
NEXP = 4
HID = 512
FT = HID // P
TILES = 4
CHUNK = TILES * P
SEQ = 256
BPC = CHUNK // SEQ
STEPS = NEXP * FT
EPS = 1e-5
ROUND = 1.5 * 2.0 ** 23
TURN = 6.283185
STAGES = 21
LEAD = 4

C_BIN, C_SFW, C_SFB, C_FB, C_FF, C_RB, C_BOUT, NCOL = 0, 3, 12, 15, 18, 21, 25, 26
X0, X1, V = 0, 1, 2


def build(nc, x, w_in, w_out, cols, fbias, filt_z, filt_mats, decay, router, w1, w3, w2,
          fwd, inv, ident, tri, out):
    ntok = x.shape[0]
    NCH = ntok // CHUNK
    NG = NCH * STEPS

    with ExitStack() as ctx:
        def sb(name, shape, dt=F32):
            return ctx.enter_context(nc.sbuf_tensor(name, shape, dt))

        def ps(name, shape=(P, 512)):
            return ctx.enter_context(nc.psum_tensor(name, list(shape), F32))

        def sem(name):
            return ctx.enter_context(nc.semaphore(name))

        x_sb = sb("x_sb", [P, NCH * TILES, P])
        cols_sb = sb("cols_sb", [P, NCOL])
        fbias_sb = sb("fbias_sb", [1, P])
        filt_z_sb = sb("filt_z_sb", [6, P + SEQ])
        filt_mats_sb = sb("filt_mats_sb", [P, 3, P])
        decay_sb = sb("decay_sb", [P, 4, P])
        ident_sb = sb("ident_sb", [P, P])
        tri_sb = sb("tri_sb", [P, NEXP * NEXP])
        fwd_sb = sb("fwd_sb", [P, 2, 2, LFILT], F32R)
        inv_sb = sb("inv_sb", [P, 2, 4, SEQ], F32R)
        w_in_sb = sb("w_in_sb", [P, 3 * P])
        w_in_hi = sb("w_in_hi", [P, 3 * P], F32R)
        w_in_lo = sb("w_in_lo", [P, 3 * P], F32R)
        w_out_sb = sb("w_out_sb", [P, P])
        w_out_hi = sb("w_out_hi", [P, P], F32R)
        w_out_lo = sb("w_out_lo", [P, P], F32R)
        router_sb = sb("router_sb", [P, NEXP])
        router_hl = sb("router_hl", [P, 2 * NEXP], F32R)
        EW_RING = 6
        ew_sb = [sb(f"ew_sb{i}", [P, HID]) for i in range(EW_RING)]
        ew_hi = [sb(f"ew{n}_hi", [P, NEXP, HID], F32R) for n in (1, 3, 2)]
        ew_lo = [sb(f"ew{n}_lo", [P, NEXP, HID], F32R) for n in (1, 3, 2)]
        tap2_bias = sb("tap2_bias", [P, 3])
        warmed = sb("warmed", [P, 1])
        fturns = sb("fturns", [P, 3])
        minus_half = sb("minus_half", [P, TILES])
        e_base = sb("e_base", [P, TILES * NEXP])

        khat_a = sb("khat_a", [P, 4, BPC, P])
        khat_b = sb("khat_b", [P, 4, BPC, P])

        kinds = ("x", "o", "x1", "moe")
        stats = {k: sb(f"stats_{k}", [P, TILES, 6]) for k in kinds}
        mv = {k: sb(f"mv_{k}", [P, TILES, 2]) for k in kinds}
        veps = {k: sb(f"veps_{k}", [P, TILES]) for k in kinds}
        rstd = {k: sb(f"rstd_{k}", [P, TILES]) for k in kinds}
        negm = {k: sb(f"negm_{k}", [P, TILES]) for k in ("o", "moe")}
        nbias = {k: sb(f"nbias_{k}", [P, TILES]) for k in ("o", "moe")}
        xn = sb("xn", [P, TILES, P])
        xnT_hi = sb("xnT_hi", [P, CHUNK], F32R)
        xnT_lo = sb("xnT_lo", [P, CHUNK], F32R)
        up = [sb(f"up{s}", [P, BPC, SEQ + 2]) for s in range(3)]
        tap2 = [sb(f"tap2_{s}", [P, BPC, SEQ]) for s in range(3)]
        uc = tap2
        vx = sb("vx", [P, BPC, SEQ])
        vT_hi = sb("vT_hi", [P, 2, BPC, P], F32R)
        vT_lo = sb("vT_lo", [P, 2, BPC, P], F32R)
        pa = sb("pa", [P, 2, 2, BPC * P])
        pb = sb("pb", [P, 2, 2, BPC * P])
        yh = pa
        yh_hi = sb("yh_hi", [P, 2, 2, BPC * P], F32R)
        yh_lo = sb("yh_lo", [P, 2, 2, BPC * P], F32R)
        gated = sb("gated", [P, CHUNK])
        gated_hi = sb("gated_hi", [P, CHUNK], F32R)
        gated_lo = sb("gated_lo", [P, CHUNK], F32R)
        oT = sb("oT", [P, CHUNK])
        o_n = sb("o_n", [P, TILES, P])
        x1 = sb("x1", [P, 2, TILES, P])
        xf = sb("xf", [P, TILES, P])
        xfT_hi = sb("xfT_hi", [P, 2, CHUNK], F32R)
        xfT_lo = sb("xfT_lo", [P, 2, CHUNK], F32R)

        lg_a = sb("lg_a", [P, TILES, NEXP])
        lg = sb("lg", [P, TILES, NEXP])
        lg_max = sb("lg_max", [P, TILES])
        lg_z = sb("lg_z", [P, TILES, NEXP])
        ge = sb("ge", [P, TILES, NEXP])
        beats = sb("beats", [P, TILES, NEXP, NEXP])
        ties = sb("ties", [P, TILES, NEXP, NEXP])
        ties_low = sb("ties_low", [P, TILES, NEXP, NEXP])
        ahead = sb("ahead", [P, TILES, NEXP, NEXP])
        place = sb("place", [P, TILES, NEXP])
        kept = sb("kept", [P, TILES, NEXP])
        ksum = sb("ksum", [P, TILES])
        krec = sb("krec", [P, TILES])
        gates = sb("gates", [P, 2, TILES, NEXP])

        silu = sb("silu", [P, 2, CHUNK])
        hid = sb("hid", [P, 2, CHUNK])
        hid_hi = sb("hid_hi", [P, 4, CHUNK], F32R)
        hid_lo = sb("hid_lo", [P, 4, CHUNK], F32R)
        fpos, fwhole, fpart, fh = (hid[:, i // 2, (i % 2) * SEQ:(i % 2 + 1) * SEQ] for i in range(4))
        taps = silu[:, 0].rearrange("p (i d) -> p i d", i=4)
        fold, fold_hi, fold_lo = (t.rearrange("p (h n) -> p h n", h=2)
                                  for t in (silu[:, 1], hid_hi[:, 0], hid_lo[:, 0]))
        eoT = sb("eoT", [P, CHUNK])
        acc = sb("acc", [P, TILES, P])
        weighted = sb("weighted", [P, TILES, P])
        acc_n = sb("acc_n", [P, TILES, P])
        y = acc_n

        ps_h1 = [ps("ps_h1a"), ps("ps_h1b")]
        ps_h3 = [ps("ps_h3a"), ps("ps_h3b")]
        ps_eo = ps("ps_eo")
        ps_et = ps("ps_et")
        ps_a = ps("ps_a")
        ps_b = ps("ps_b")

        ld_x = [sem(f"ld_x{c}") for c in range(NCH)]
        ld = {k: sem(f"ld_{k}") for k in ("cols", "fbias", "fz", "fmats", "decay", "ident", "tri",
                                         "w_in", "w_out", "router", "fwd", "inv")}
        ld_ew = [[sem(f"ld_ew{m}_{e}") for e in range(NEXP)] for m in range(3)]
        stored = sem("stored")
        consts_set = sem("consts_set")
        pads_set = sem("pads_set")
        ew_hi_done = sem("ew_hi_done")
        ew_lo_done = sem("ew_lo_done")
        w_in_hi_done = sem("w_in_hi_done")
        w_in_lo_done = sem("w_in_lo_done")
        w_out_hi_done = sem("w_out_hi_done")
        w_out_lo_done = sem("w_out_lo_done")
        tap2_bias_a = sem("tap2_bias_a")
        tap2_bias_done = sem("tap2_bias_done")
        f_mm = sem("f_mm")
        fturns_done = sem("fturns_done")
        tables_warm = sem("tables_warm")
        f_pos = sem("f_pos")
        f_whole = sem("f_whole")
        f_part = sem("f_part")
        f_sin = sem("f_sin")
        taps_mm = sem("taps_mm")
        taps_done = sem("taps_done")
        fold_done = sem("fold_done")
        fold_hi_done = sem("fold_hi_done")
        fold_lo_done = sem("fold_lo_done")
        khat_mm = sem("khat_mm")
        khat_even_copied = sem("khat_even_copied")
        khat_even_done = sem("khat_even_done")
        khat_zeroed = sem("khat_zeroed")
        khat_odd_done = sem("khat_odd_done")
        ln_stats = {k: sem(f"ln_stats_{k}") for k in kinds}
        ln_mv = {k: sem(f"ln_mv_{k}") for k in kinds}
        ln_veps = {k: sem(f"ln_veps_{k}") for k in kinds}
        ln_rstd = {k: sem(f"ln_rstd_{k}") for k in kinds}
        ln_nbias = {k: sem(f"ln_nbias_{k}") for k in ("o", "moe")}
        xn_done = sem("xn_done")
        xnT_mm = sem("xnT_mm")
        xnT_hi_done = sem("xnT_hi_done")
        xnT_lo_done = sem("xnT_lo_done")
        proj_mm = [sem(f"proj_mm{s}") for s in range(3)]
        up_done = [sem(f"up_done{s}") for s in range(3)]
        tap2_done = [sem(f"tap2_done{s}") for s in range(3)]
        tap1_done = [sem(f"tap1_done{s}") for s in range(3)]
        uc_done = [sem(f"uc_done{s}") for s in range(3)]
        vx_done = sem("vx_done")
        vT_mm = sem("vT_mm")
        vT_hi_done = sem("vT_hi_done")
        vT_lo_done = sem("vT_lo_done")
        fwd_mm = [sem("fwd_mm_even"), sem("fwd_mm_odd")]
        prod_a = [sem("prod_a_even"), sem("prod_a_odd")]
        prod_b = [sem("prod_b_even"), sem("prod_b_odd")]
        yh_done = [sem("yh_done_even"), sem("yh_done_odd")]
        yh_hi_done = [sem("yh_hi_even"), sem("yh_hi_odd")]
        yh_lo_done = [sem("yh_lo_even"), sem("yh_lo_odd")]
        y_mm = sem("y_mm")
        gated_done = sem("gated_done")
        gated_hi_done = sem("gated_hi_done")
        gated_lo_done = sem("gated_lo_done")
        oT_mm = sem("oT_mm")
        oT_done = sem("oT_done")
        o_mm = sem("o_mm")
        o_n_done = sem("o_n_done")
        x1_done = sem("x1_done")
        xf_done = sem("xf_done")
        xfT_mm = sem("xfT_mm")
        xfT_hi_done = sem("xfT_hi_done")
        xfT_lo_done = sem("xfT_lo_done")
        router_hi_done = sem("router_hi_done")
        router_lo_done = sem("router_lo_done")
        logits_mm = sem("logits_mm")
        lg_a_done = sem("lg_a_done")
        lg_done = sem("lg_done")
        lg_max_done = sem("lg_max_done")
        lg_z_done = sem("lg_z_done")
        ge_done = sem("ge_done")
        beats_done = sem("beats_done")
        ties_done = sem("ties_done")
        ties_low_done = sem("ties_low_done")
        ahead_done = sem("ahead_done")
        place_done = sem("place_done")
        kept_done = sem("kept_done")
        ksum_done = sem("ksum_done")
        krec_done = sem("krec_done")
        gates_done = sem("gates_done")
        h1_mm = sem("h1_mm")
        h3_mm = sem("h3_mm")
        silu_done = sem("silu_done")
        hid_done = sem("hid_done")
        hid_hi_done = sem("hid_hi_done")
        hid_lo_done = sem("hid_lo_done")
        eo_mm = sem("eo_mm")
        eoT_done = sem("eoT_done")
        et_mm = sem("et_mm")
        weighted_done = sem("weighted_done")
        acc_first = sem("acc_first")
        acc_added = sem("acc_added")
        acc_n_done = sem("acc_n_done")
        y_done = sem("y_done")

        block = ctx.enter_context(nc.Block())

        x_dram = x.rearrange("(t p) d -> p t d", p=P)
        out_dram = out.rearrange("(t p) d -> p t d", p=P)
        ew_dram = [w1.rearrange("e d f -> d e f"), w3.rearrange("e d f -> d e f"),
                   w2.rearrange("e (j f) d -> f e j d", f=P)]

        FIRST, LAST = -STEPS - LEAD, NG + 6

        def hyena_at(g):
            for c in range(NCH):
                stage = g - (STEPS * (c - 1) - LEAD)
                if 0 <= stage < STAGES:
                    yield c, stage

        @block.sync
        def _(sp):
            sp.dma_start(x_sb[:, 0:TILES, :], x_dram[:, 0:TILES, :]).then_inc(ld_x[0], 16)
            sp.dma_start(w_in_sb[:], w_in).then_inc(ld["w_in"], 16)
            sp.dma_start(decay_sb[:], decay).then_inc(ld["decay"], 16)
            for e in range(NEXP):
                for m in range(3):
                    i = 3 * e + m
                    dst = ew_sb[i % EW_RING][:]
                    src = ew_dram[m][:, e]
                    if i >= EW_RING:
                        sp.wait_ge(ew_lo_done, i - EW_RING + 1)
                    if m == 2:
                        dst = dst.rearrange("p (j d) -> p j d", j=FT)
                    sp.dma_start(dst, src).then_inc(ld_ew[m][e], 16)
                if e + 1 < NCH:
                    c = e + 1
                    sp.dma_start(x_sb[:, c * TILES:(c + 1) * TILES, :],
                                 x_dram[:, c * TILES:(c + 1) * TILES, :]).then_inc(ld_x[c], 16)
            for c in range(NCH):
                sp.wait_ge(y_done, c + 1)
                sp.dma_start(out_dram[:, c * TILES:(c + 1) * TILES, :], y[:]).then_inc(stored, 16)
            sp.wait_ge(stored, 16 * NCH)

        @block.gpsimd
        def _(pool):
            pool.dma_start(fwd_sb[:], fwd).then_inc(ld["fwd"], 16)
            pool.dma_start(inv_sb[:], inv).then_inc(ld["inv"], 16)
            nc.gpsimd.memset(minus_half[:], -0.5).then_inc(consts_set, 1)
            nc.gpsimd.memset(e_base[:], float(np.exp(1.0))).then_inc(consts_set, 1)
            for s in range(3):
                nc.gpsimd.memset(up[s][:, :, 0:2], 0.0).then_inc(pads_set, 1)

            def inv_std(kind, c):
                pool.wait_ge(ln_mv[kind], TILES * (c + 1))
                nc.gpsimd.tensor_scalar(veps[kind][:], mv[kind][:, :, 1], EPS, None,
                                        ALU.add).then_inc(ln_veps[kind], 1)
                if kind in negm:
                    nc.gpsimd.tensor_scalar(negm[kind][:], mv[kind][:, :, 0], -1.0, None,
                                            ALU.mult).then_inc(ln_veps[kind], 1)
                pool.wait_ge(ln_veps[kind], (2 if kind in negm else 1) * (c + 1))
                if c == 0:
                    pool.wait_ge(consts_set, 2)
                nc.gpsimd.tensor_tensor(rstd[kind][:], veps[kind][:], minus_half[:],
                                        ALU.pow).then_inc(ln_rstd[kind], 1)
                pool.wait_ge(ln_rstd[kind], c + 1)
                if kind in negm:
                    nc.gpsimd.tensor_tensor(nbias[kind][:], negm[kind][:], rstd[kind][:],
                                            ALU.mult).then_inc(ln_nbias[kind], 1)

            def split_expert(e):
                for m in range(3):
                    i = 3 * e + m
                    pool.wait_ge(ew_hi_done, i + 1)
                    nc.gpsimd.tensor_tensor(ew_lo[m][:, e, :], ew_sb[i % EW_RING][:],
                                            ew_hi[m][:, e, :].bitcast(F32),
                                            ALU.subtract).then_inc(ew_lo_done, 1)

            def hyena(c, stage):
                if stage == 0:
                    inv_std("x", c)
                if stage == 3 and c == 0:
                    split_expert(0)
                if stage == 5:
                    pool.wait_ge(uc_done[X1], c + 1)
                    pool.wait_ge(uc_done[V], c + 1)
                    nc.gpsimd.tensor_tensor(vx[:], uc[V][:], uc[X1][:], ALU.mult).then_inc(vx_done, 1)
                    if c == 0:
                        split_expert(1)
                if stage == 8:
                    if c == 0:
                        pool.wait_ge(khat_even_copied, 3)
                        nc.gpsimd.memset(khat_b[0:1, 0:2], 0.0).then_inc(khat_zeroed, 1)
                    pool.wait_ge(prod_a[0], c + 1)
                    pool.wait_ge(prod_b[0], c + 1)
                    nc.gpsimd.tensor_tensor(yh[:, 0], pa[:, 0], pb[:, 0], ALU.add).then_inc(yh_done[0], 1)
                if stage == 9:
                    pool.wait_ge(yh_hi_done[0], c + 1)
                    nc.gpsimd.tensor_tensor(yh_lo[:, 0], yh[:, 0], yh_hi[:, 0].bitcast(F32),
                                            ALU.subtract).then_inc(yh_lo_done[0], 1)
                    if c == 0:
                        split_expert(2)
                if stage == 11:
                    pool.wait_ge(gated_hi_done, c + 1)
                    nc.gpsimd.tensor_tensor(gated_lo[:], gated[:], gated_hi[:].bitcast(F32),
                                            ALU.subtract).then_inc(gated_lo_done, 1)
                    if c == 0:
                        split_expert(3)
                if stage == 14:
                    inv_std("o", c)
                if stage == 16:
                    inv_std("x1", c)
                if stage == 19:
                    pool.wait_ge(lg_z_done, c + 1)
                    nc.gpsimd.tensor_tensor(ge[:], e_base[:].rearrange("p (t e) -> p t e", e=NEXP),
                                            lg_z[:], ALU.pow).then_inc(ge_done, 1)

            for g in range(FIRST, LAST):
                if g >= 7 and (g - 7) % FT == 0:
                    n = (g - 7) // FT
                    c, e = divmod(n, NEXP)
                    if c < NCH and e > 0:
                        added = 3 * c + e
                        pool.wait_ge(weighted_done, added)
                        pool.wait_ge(acc_first, c + 1)
                        if e > 1:
                            pool.wait_ge(acc_added, added - 1)
                        nc.gpsimd.tensor_tensor(acc[:], acc[:], weighted[:], ALU.add).then_inc(acc_added, 1)
                if g >= STEPS and (g - 4) % STEPS == 0:
                    inv_std("moe", g // STEPS - 1)
                for c, stage in hyena_at(g):
                    hyena(c, stage)

        @block.tensor
        def _(pe):
            def product(dst, a_hi, a_lo, b_hi, b_lo, start=True, stop=True):
                nc.tensor.matmul(dst, a_hi, b_hi, start=start, stop=False)
                nc.tensor.matmul(dst, a_lo, b_hi, start=False, stop=False)
                return nc.tensor.matmul(dst, a_hi, b_lo, start=False, stop=stop)

            def transposes(dst, tile_of):
                for j in range(TILES):
                    last = nc.tensor.transpose(dst[:, j * P:(j + 1) * P], tile_of(j), ident_sb[:])
                return last

            def projection(c, s, bank):
                for n in range(3):
                    a = (w_in_hi, w_in_lo, w_in_hi)[n][:, s * P:(s + 1) * P]
                    b = (xnT_hi, xnT_hi, xnT_lo)[n][:]
                    if n == 2:
                        pe.wait_ge(xnT_lo_done, c + 1)
                    last = nc.tensor.matmul(bank[:], a, b, start=(n == 0), stop=(n == 2))
                last.then_inc(proj_mm[s], 1)

            def transform(c, half, bank):
                for i in range(2):
                    f0 = (2 * half + i) * P
                    for kt in range(2):
                        last = product(bank[:, i * BPC * P:(i + 1) * BPC * P],
                                       fwd_sb[:, 0, kt, f0:f0 + P], fwd_sb[:, 1, kt, f0:f0 + P],
                                       vT_hi[:, kt].rearrange("p b d -> p (b d)"),
                                       vT_lo[:, kt].rearrange("p b d -> p (b d)"),
                                       start=(kt == 0), stop=(kt == 1))
                last.then_inc(fwd_mm[half], 1)

            def filter_layer(n):
                bank = (ps_h1[0], ps_h1[1], ps_h3[0])[n]
                if n == 0:
                    pe.wait_ge(ld["fz"], 16)
                    last = nc.tensor.matmul(bank[:, 0:SEQ], filt_z_sb[:, 0:P], filt_z_sb[:, P:P + SEQ],
                                            start=True, stop=True)
                else:
                    if n == 1:
                        pe.wait_ge(ld["fmats"], 16)
                    pe.wait_ge(f_sin, n)
                    last = nc.tensor.matmul(bank[:, 0:SEQ], filt_mats_sb[:, n - 1, :], fh,
                                            start=True, stop=True)
                last.then_inc(f_mm, 1)

            def filter_taps():
                pe.wait_ge(f_sin, 3)
                half = P // 2
                for i in range(4):
                    h = i // 2
                    bank = (ps_h3[1], ps_et)[h]
                    last = nc.tensor.matmul(bank[:, (i % 2) * P:(i % 2 + 1) * P],
                                            fh[h * half:(h + 1) * half, (i % 2) * P:(i % 2 + 1) * P],
                                            filt_mats_sb[h * half:(h + 1) * half, 2, :],
                                            start=True, stop=True)
                    if i % 2:
                        last.then_inc(taps_mm, 1)

            def filter_transform():
                pe.wait_ge(ld["fwd"], 16)
                pe.wait_ge(fold_hi_done, 1)
                pe.wait_ge(fold_lo_done, 1)
                for i in range(4):
                    bank = (ps_eo, ps_et)[i // 2]
                    for kt in range(2):
                        last = product(bank[:, (i % 2) * P:(i % 2 + 1) * P],
                                       fwd_sb[:, 0, kt, i * P:(i + 1) * P],
                                       fwd_sb[:, 1, kt, i * P:(i + 1) * P],
                                       fold_hi[:, i // 2, kt * P:(kt + 1) * P],
                                       fold_lo[:, i // 2, kt * P:(kt + 1) * P],
                                       start=(kt == 0), stop=(kt == 1))
                    if i % 2:
                        last.then_inc(khat_mm, 1)

            def hyena(c, stage):
                if stage == 0 and c == 0:
                    filter_layer(0)
                if stage == 2:
                    if c == 0:
                        pe.wait_ge(ld["ident"], 16)
                    pe.wait_ge(xn_done, TILES * (c + 1))
                    if c > 0:
                        pe.wait_ge(xfT_lo_done, c)
                    transposes(ps_a, lambda j: xn[:, j, :]).then_inc(xnT_mm, 1)
                    if c == 0:
                        filter_layer(1)
                if stage == 3:
                    if c == 0:
                        pe.wait_ge(w_in_hi_done, 1)
                        pe.wait_ge(w_in_lo_done, 1)
                    pe.wait_ge(xnT_hi_done, c + 1)
                    if c > 0:
                        pe.wait_ge(lg_done, c)
                    projection(c, X1, ps_b)
                if stage == 4:
                    projection(c, V, ps_a)
                    if c == 0:
                        filter_layer(2)
                if stage == 5:
                    pe.wait_ge(up_done[X1], c + 1)
                    pe.wait_ge(tap2_done[X1], c + 1)
                    projection(c, X0, ps_b)
                    if c == 0:
                        filter_taps()
                if stage == 7:
                    pe.wait_ge(up_done[V], c + 1)
                    pe.wait_ge(tap2_done[V], c + 1)
                    pe.wait_ge(vx_done, c + 1)
                    for kt in range(2):
                        for b in range(BPC):
                            at = (kt * BPC + b) * P
                            last = nc.tensor.transpose(ps_a[:, at:at + P], vx[:, b, kt * P:(kt + 1) * P],
                                                       ident_sb[:])
                    last.then_inc(vT_mm, 1)
                    if c == 0:
                        filter_transform()
                if stage == 8:
                    if c == 0:
                        pe.wait_ge(ld["fwd"], 16)
                    pe.wait_ge(up_done[X0], c + 1)
                    pe.wait_ge(tap2_done[X0], c + 1)
                    pe.wait_ge(vT_hi_done, c + 1)
                    pe.wait_ge(vT_lo_done, c + 1)
                    transform(c, 0, ps_b)
                if stage == 9:
                    transform(c, 1, ps_a)
                if stage == 11:
                    if c == 0:
                        pe.wait_ge(ld["inv"], 16)
                    for h in range(2):
                        pe.wait_ge(yh_hi_done[h], c + 1)
                        pe.wait_ge(yh_lo_done[h], c + 1)
                    for b in range(BPC):
                        for i in range(4):
                            hi = yh_hi[:, i // 2, i % 2, b * P:(b + 1) * P]
                            lo = yh_lo[:, i // 2, i % 2, b * P:(b + 1) * P]
                            last = product(ps_b[:, b * SEQ:(b + 1) * SEQ], hi, lo,
                                           inv_sb[:, 0, i, :], inv_sb[:, 1, i, :],
                                           start=(i == 0), stop=(i == 3))
                    last.then_inc(y_mm, 1)
                if stage == 13:
                    if c == 0:
                        pe.wait_ge(w_out_hi_done, 1)
                        pe.wait_ge(w_out_lo_done, 1)
                    pe.wait_ge(gated_hi_done, c + 1)
                    pe.wait_ge(gated_lo_done, c + 1)
                    product(ps_a[:], w_out_hi[:], w_out_lo[:], gated_hi[:], gated_lo[:]).then_inc(oT_mm, 1)
                if stage == 14:
                    pe.wait_ge(oT_done, c + 1)
                    transposes(ps_b, lambda j: oT[:, j * P:(j + 1) * P]).then_inc(o_mm, 1)
                if stage == 18:
                    pe.wait_ge(xf_done, TILES * (c + 1))
                    transposes(ps_a, lambda j: xf[:, j, :]).then_inc(xfT_mm, 1)
                if stage == 19:
                    if c == 0:
                        pe.wait_ge(router_hi_done, 1)
                        pe.wait_ge(router_lo_done, 1)
                    pe.wait_ge(xfT_hi_done, c + 1)
                    pe.wait_ge(xfT_lo_done, c + 1)
                    pe.wait_ge(o_n_done, TILES * (c + 1))
                    for j in range(TILES):
                        t = slice(j * P, (j + 1) * P)
                        dst = ps_b[:, j * 2 * NEXP:(j + 1) * 2 * NEXP]
                        nc.tensor.matmul(dst, xfT_hi[:, c % 2, t], router_hl[:], start=True, stop=False)
                        last = nc.tensor.matmul(dst, xfT_lo[:, c % 2, t], router_hl[:], start=False, stop=True)
                    last.then_inc(logits_mm, 1)

            def up_products(g):
                c, k = divmod(g, STEPS)
                e, f = divmod(k, FT)
                if k == 0:
                    pe.wait_ge(xfT_hi_done, c + 1)
                    pe.wait_ge(xfT_lo_done, c + 1)
                if c == 0 and f == 0:
                    pe.wait_ge(ew_lo_done, 3 * e + 2)
                fs = slice(f * P, (f + 1) * P)
                if g >= 2:
                    pe.wait_ge(silu_done, g - 1)
                product(ps_h1[g % 2][:], ew_hi[0][:, e, fs], ew_lo[0][:, e, fs],
                        xfT_hi[:, c % 2], xfT_lo[:, c % 2]).then_inc(h1_mm, 1)
                if g >= 2:
                    pe.wait_ge(hid_done, g - 1)
                product(ps_h3[g % 2][:], ew_hi[1][:, e, fs], ew_lo[1][:, e, fs],
                        xfT_hi[:, c % 2], xfT_lo[:, c % 2]).then_inc(h3_mm, 1)

            def down_product(g):
                c, k = divmod(g, STEPS)
                e, f = divmod(k, FT)
                if c == 0 and f == 0:
                    pe.wait_ge(ew_lo_done, 3 * e + 3)
                if f == 0 and g > 0:
                    pe.wait_ge(eoT_done, g // FT)
                pe.wait_ge(hid_hi_done, g + 1)
                pe.wait_ge(hid_lo_done, g + 1)
                fs = slice(f * P, (f + 1) * P)
                product(ps_eo[:], ew_hi[2][:, e, fs], ew_lo[2][:, e, fs], hid_hi[:, g % 4], hid_lo[:, g % 4],
                        start=(f == 0), stop=(f == FT - 1)).then_inc(eo_mm, 1)

            for g in range(FIRST, LAST):
                if 0 <= g < NG:
                    up_products(g)
                if 0 <= g - 2 < NG:
                    down_product(g - 2)
                if g >= 6 and (g - 6) % FT == 0 and (g - 6) // FT < NG // FT:
                    n = (g - 6) // FT
                    pe.wait_ge(eoT_done, n + 1)
                    if n > 0:
                        last_c, last_e = divmod(n - 1, NEXP)
                        if last_e == 0:
                            pe.wait_ge(acc_first, last_c + 1)
                        else:
                            pe.wait_ge(weighted_done, 3 * last_c + last_e)
                    transposes(ps_et, lambda j: eoT[:, j * P:(j + 1) * P]).then_inc(et_mm, 1)
                for c, stage in hyena_at(g):
                    hyena(c, stage)

        @block.scalar
        def _(act):
            act.dma_start(filt_z_sb[:], filt_z).then_inc(ld["fz"], 16)
            act.dma_start(cols_sb[:], cols).then_inc(ld["cols"], 16)
            act.dma_start(filt_mats_sb[:], filt_mats).then_inc(ld["fmats"], 16)
            act.dma_start(ident_sb[:], ident).then_inc(ld["ident"], 16)
            act.dma_start(fbias_sb[:], fbias).then_inc(ld["fbias"], 16)
            act.dma_start(w_out_sb[:], w_out).then_inc(ld["w_out"], 16)
            act.dma_start(router_sb[:], router).then_inc(ld["router"], 16)
            act.dma_start(tri_sb[:], tri).then_inc(ld["tri"], 16)

            act.wait_ge(consts_set, 2)
            nc.scalar.activation(warmed[:], minus_half[:, 0:1], ACT.Silu).then_inc(tables_warm, 1)

            def filter_sin(n):
                act.wait_ge(f_part, n + 1)
                nc.scalar.activation(fh, fpart, ACT.Sin, scale=TURN).then_inc(f_sin, 1)

            def split_expert(e):
                for m in range(3):
                    act.wait_ge(ld_ew[m][e], 16)
                    nc.scalar.activation(ew_hi[m][:, e, :], ew_sb[(3 * e + m) % EW_RING][:],
                                         ACT.Copy).then_inc(ew_hi_done, 1)

            def khat_even():
                act.wait_ge(khat_mm, 1)

                def times(i, n):
                    return ps_eo[:, i * P:(i + 1) * P].unsqueeze(1).broadcast_to([P, n, P])
                nc.scalar.activation(khat_a[:, 0:2].rearrange("p i b d -> p (i b) d"), times(0, 2 * BPC),
                                     ACT.Copy).then_inc(khat_even_copied, 1)
                for i, sign in enumerate((-1.0, 1.0)):
                    nc.scalar.activation(khat_b[:, i], times(1, BPC), ACT.Copy,
                                         scale=sign).then_inc(khat_even_copied, 1)
                act.wait_ge(khat_even_copied, 3)
                nc.scalar.activation(khat_a[0:1, 1], times(1, BPC)[0:1], ACT.Copy).then_inc(khat_even_done, 1)

            def up_and_tap2(c, s, bank):
                act.wait_ge(proj_mm[s], c + 1)
                src = bank[:].rearrange("p (b t) -> p b t", b=BPC)
                if c > 0:
                    act.wait_ge(uc_done[s], c)
                nc.scalar.activation(up[s][:, :, 2:], src, ACT.Identity,
                                     bias=cols_sb[:, C_BIN + s:C_BIN + s + 1]).then_inc(up_done[s], 1)
                nc.scalar.activation(tap2[s][:], src, ACT.Identity,
                                     scale=cols_sb[:, C_SFW + 3 * s + 2:C_SFW + 3 * s + 3],
                                     bias=tap2_bias[:, s:s + 1]).then_inc(tap2_done[s], 1)

            def normed(kind, c, dst, src, done):
                act.wait_ge(ln_nbias[kind], c + 1)
                for j in range(TILES):
                    nc.scalar.activation(dst[:, j, :], src(j), ACT.Identity, bias=nbias[kind][:, j:j + 1],
                                         scale=rstd[kind][:, j:j + 1]).then_inc(done, 1)

            def hyena(c, stage):
                if stage == 0 and c == 0:
                    filter_sin(0)
                    act.wait_ge(ld["w_in"], 16)
                    nc.scalar.activation(w_in_hi[:], w_in_sb[:], ACT.Copy).then_inc(w_in_hi_done, 1)
                if stage == 2:
                    act.wait_ge(xnT_mm, c + 1)
                    nc.scalar.activation(xnT_hi[:], ps_a[:], ACT.Copy).then_inc(xnT_hi_done, 1)
                    if c == 0:
                        filter_sin(1)
                        act.wait_ge(tap2_bias_done, 1)
                        act.wait_ge(pads_set, 3)
                        split_expert(0)
                if stage == 3:
                    up_and_tap2(c, X1, ps_b)
                if stage == 4:
                    up_and_tap2(c, V, ps_a)
                    if c == 0:
                        filter_sin(2)
                if stage == 5:
                    up_and_tap2(c, X0, ps_b)
                    if c == 0:
                        split_expert(1)
                if stage == 6 and c == 0:
                    act.wait_ge(fold_done, 2)
                    nc.scalar.activation(fold_hi, fold, ACT.Copy).then_inc(fold_hi_done, 1)
                if stage == 7:
                    act.wait_ge(vT_mm, c + 1)
                    nc.scalar.activation(vT_hi[:].rearrange("p k b d -> p (k b d)"), ps_a[:],
                                         ACT.Copy).then_inc(vT_hi_done, 1)
                    if c == 0:
                        khat_even()
                if stage in (9, 10):
                    h = stage - 9
                    act.wait_ge(yh_done[h], c + 1)
                    nc.scalar.activation(yh_hi[:, h], yh[:, h], ACT.Copy).then_inc(yh_hi_done[h], 1)
                if stage == 10 and c == 0:
                    act.wait_ge(ld["w_out"], 16)
                    nc.scalar.activation(w_out_hi[:], w_out_sb[:], ACT.Copy).then_inc(w_out_hi_done, 1)
                    act.wait_ge(ld["router"], 16)
                    nc.scalar.activation(router_hl[:, 0:NEXP], router_sb[:], ACT.Copy).then_inc(router_hi_done, 1)
                    split_expert(2)
                if stage == 11:
                    act.wait_ge(gated_done, c + 1)
                    nc.scalar.activation(gated_hi[:], gated[:], ACT.Copy).then_inc(gated_hi_done, 1)
                    if c == 0:
                        split_expert(3)
                if stage == 13:
                    act.wait_ge(oT_mm, c + 1)
                    nc.scalar.activation(oT[:], ps_a[:], ACT.Identity,
                                         bias=cols_sb[:, C_BOUT:C_BOUT + 1]).then_inc(oT_done, 1)
                if stage == 15:
                    if c > 0:
                        act.wait_ge(x1_done, c)
                    normed("o", c, o_n, lambda j: ps_b[:, j * P:(j + 1) * P], o_n_done)
                if stage == 18:
                    act.wait_ge(xfT_mm, c + 1)
                    nc.scalar.activation(xfT_hi[:, c % 2], ps_a[:], ACT.Copy).then_inc(xfT_hi_done, 1)

            for g in range(FIRST, LAST):
                if 0 <= g < NG:
                    act.wait_ge(h1_mm, g + 1)
                    if g >= 2:
                        act.wait_ge(hid_done, g - 1)
                    nc.scalar.activation(silu[:, g % 2], ps_h1[g % 2][:], ACT.Silu).then_inc(silu_done, 1)
                if 0 <= g - 1 < NG:
                    act.wait_ge(hid_done, g)
                    nc.scalar.activation(hid_hi[:, (g - 1) % 4], hid[:, (g - 1) % 2],
                                         ACT.Copy).then_inc(hid_hi_done, 1)
                if g >= 5 and (g - 5) % FT == 0 and (g - 5) // FT < NG // FT:
                    n = (g - 5) // FT
                    act.wait_ge(eo_mm, FT * (n + 1))
                    if n > 0:
                        act.wait_ge(et_mm, n)
                    nc.scalar.activation(eoT[:], ps_eo[:], ACT.Copy).then_inc(eoT_done, 1)
                if g >= STEPS and (g - 5) % STEPS == 0:
                    if g // STEPS >= 2:
                        act.wait_ge(stored, 16 * (g // STEPS - 1))
                    normed("moe", g // STEPS - 1, acc_n, lambda j: acc[:, j, :], acc_n_done)
                for c, stage in hyena_at(g):
                    hyena(c, stage)

        @block.vector
        def _(dve):
            def moments(kind, c, src):
                for j in range(TILES):
                    nc.vector.bn_stats(stats[kind][:, j, :], src(j)).then_inc(ln_stats[kind], 1)
                for j in range(TILES):
                    dve.wait_ge(ln_stats[kind], TILES * c + j + 1)
                    nc.vector.bn_aggr(mv[kind][:, j, :], stats[kind][:, j, :]).then_inc(ln_mv[kind], 1)

            def filter_reduce(n):
                bank = (ps_h1[0], ps_h1[1], ps_h3[0])[n]
                dve.wait_ge(f_mm, n + 1)
                nc.vector.tensor_scalar(fpos, bank[:, 0:SEQ], cols_sb[:, C_FB + n:C_FB + n + 1],
                                        fturns[:, n:n + 1], ALU.add, ALU.mult).then_inc(f_pos, 1)
                dve.wait_ge(f_pos, n + 1)
                nc.vector.tensor_scalar(fwhole, fpos, ROUND, ROUND, ALU.add, ALU.subtract).then_inc(f_whole, 1)
                dve.wait_ge(f_whole, n + 1)
                if n > 0:
                    dve.wait_ge(f_sin, n)
                nc.vector.tensor_tensor(fpart, fpos, fwhole, ALU.subtract).then_inc(f_part, 1)

            def normalise(kind, c, dst, src, done):
                dve.wait_ge(ln_rstd[kind], c + 1)
                for j in range(TILES):
                    nc.vector.tensor_scalar(dst[:, j, :], src(j), mv[kind][:, j, 0:1], rstd[kind][:, j:j + 1],
                                            ALU.subtract, ALU.mult).then_inc(done, 1)

            def filter_fold():
                dve.wait_ge(taps_mm, 2)
                dve.wait_ge(ld["decay"], 16)
                for h, bank in enumerate((ps_h3[1], ps_et)):
                    nc.vector.tensor_tensor(taps[:, 2 * h:2 * h + 2].rearrange("p i d -> p (i d)"), bank[:, 0:2 * P],
                                            decay_sb[:, 2 * h:2 * h + 2].rearrange("p i d -> p (i d)"),
                                            ALU.mult).then_inc(taps_done, 1)
                dve.wait_ge(taps_done, 2)
                dve.wait_ge(ld["fbias"], 16)
                nc.vector.tensor_tensor(taps[0:1, 0, :], taps[0:1, 0, :], fbias_sb[:],
                                        ALU.add).then_inc(taps_done, 1)
                dve.wait_ge(taps_done, 3)
                for h, op in enumerate((ALU.add, ALU.subtract)):
                    nc.vector.tensor_tensor(fold[:, h], taps[:, 0:2].rearrange("p i d -> p (i d)"),
                                            taps[:, 2:4].rearrange("p i d -> p (i d)"), op).then_inc(fold_done, 1)
                dve.wait_ge(fold_hi_done, 1)
                nc.vector.tensor_tensor(fold_lo, fold, fold_hi.bitcast(F32),
                                        ALU.subtract).then_inc(fold_lo_done, 1)

            def short_conv(c, s):
                src = up[s]
                dve.wait_ge(up_done[s], c + 1)
                dve.wait_ge(tap2_done[s], c + 1)
                nc.vector.scalar_tensor_tensor(out=uc[s][:], in0=src[:, :, 1:SEQ + 1],
                                               scalar=cols_sb[:, C_SFW + 3 * s + 1:C_SFW + 3 * s + 2],
                                               in1=tap2[s][:], op0=ALU.mult, op1=ALU.add).then_inc(tap1_done[s], 1)
                dve.wait_ge(tap1_done[s], c + 1)
                nc.vector.scalar_tensor_tensor(out=uc[s][:], in0=src[:, :, 0:SEQ],
                                               scalar=cols_sb[:, C_SFW + 3 * s:C_SFW + 3 * s + 1],
                                               in1=uc[s][:], op0=ALU.mult, op1=ALU.add).then_inc(uc_done[s], 1)

            def spectrum_product(c, h, bank):
                dve.wait_ge(fwd_mm[h], c + 1)
                src = bank[:].rearrange("p (i n) -> p i n", i=2)
                ka = khat_a[:, 2 * h:2 * h + 2].rearrange("p i b d -> p i (b d)")
                kb = khat_b[:, 2 * h:2 * h + 2].rearrange("p i b d -> p i (b d)")
                nc.vector.tensor_tensor(pa[:, h], src, ka, ALU.mult).then_inc(prod_a[h], 1)
                nc.vector.tensor_tensor(pb[:, h], src[:, ::-1], kb, ALU.mult).then_inc(prod_b[h], 1)

            def khat_odd():
                dve.wait_ge(khat_mm, 2)

                def times(i, n):
                    return ps_et[:, i * P:(i + 1) * P].unsqueeze(1).broadcast_to([P, n, P])
                nc.vector.tensor_copy(khat_a[:, 2:4].rearrange("p i b d -> p (i b) d"),
                                      times(0, 2 * BPC)).then_inc(khat_odd_done, 1)
                for i, sign in enumerate((-1.0, 1.0)):
                    nc.vector.tensor_scalar(khat_b[:, 2 + i], times(1, BPC), sign, None,
                                            ALU.mult).then_inc(khat_odd_done, 1)

            def hyena(c, stage):
                if stage == 0:
                    dve.wait_ge(ld_x[c], 16)
                    moments("x", c, lambda j: x_sb[:, c * TILES + j, :])
                    if c == 0:
                        dve.wait_ge(ld["cols"], 16)
                        nc.vector.tensor_scalar(fturns[:], cols_sb[:, C_FF:C_FF + 3], 0.5 / np.pi, None,
                                                ALU.mult).then_inc(fturns_done, 1)
                        tap_w2 = cols_sb[:, C_SFW:C_SFW + 9].rearrange("p (s k) -> p s k", k=3)[:, :, 2]
                        nc.vector.tensor_tensor(tap2_bias[:], tap_w2, cols_sb[:, C_BIN:C_BIN + 3],
                                                ALU.mult).then_inc(tap2_bias_a, 1)
                        dve.wait_ge(fturns_done, 1)
                        filter_reduce(0)
                        dve.wait_ge(tap2_bias_a, 1)
                        nc.vector.tensor_tensor(tap2_bias[:], tap2_bias[:], cols_sb[:, C_SFB:C_SFB + 3],
                                                ALU.add).then_inc(tap2_bias_done, 1)
                        dve.wait_ge(w_in_hi_done, 1)
                        nc.vector.tensor_tensor(w_in_lo[:], w_in_sb[:], w_in_hi[:].bitcast(F32),
                                                ALU.subtract).then_inc(w_in_lo_done, 1)
                if stage == 1:
                    normalise("x", c, xn, lambda j: x_sb[:, c * TILES + j, :], xn_done)
                if stage == 2:
                    dve.wait_ge(xnT_hi_done, c + 1)
                    nc.vector.tensor_tensor(xnT_lo[:], ps_a[:], xnT_hi[:].bitcast(F32),
                                            ALU.subtract).then_inc(xnT_lo_done, 1)
                    if c == 0:
                        filter_reduce(1)
                if stage == 4:
                    if c == 0:
                        filter_reduce(2)
                    short_conv(c, X1)
                if stage == 5:
                    short_conv(c, V)
                if stage == 6:
                    if c == 0:
                        filter_fold()
                    short_conv(c, X0)
                if stage == 7:
                    dve.wait_ge(vT_hi_done, c + 1)
                    nc.vector.tensor_tensor(vT_lo[:].rearrange("p k b d -> p (k b d)"), ps_a[:],
                                            vT_hi[:].rearrange("p k b d -> p (k b d)").bitcast(F32),
                                            ALU.subtract).then_inc(vT_lo_done, 1)
                    if c == 0:
                        khat_odd()
                if stage == 8:
                    if c == 0:
                        dve.wait_ge(khat_even_done, 1)
                        dve.wait_ge(khat_zeroed, 1)
                    spectrum_product(c, 0, ps_b)
                if stage == 9:
                    if c == 0:
                        dve.wait_ge(khat_odd_done, 3)
                    spectrum_product(c, 1, ps_a)
                    dve.wait_ge(prod_a[1], c + 1)
                    dve.wait_ge(prod_b[1], c + 1)
                    nc.vector.tensor_tensor(yh[:, 1], pa[:, 1], pb[:, 1], ALU.add).then_inc(yh_done[1], 1)
                if stage == 10:
                    dve.wait_ge(yh_hi_done[1], c + 1)
                    nc.vector.tensor_tensor(yh_lo[:, 1], yh[:, 1], yh_hi[:, 1].bitcast(F32),
                                            ALU.subtract).then_inc(yh_lo_done[1], 1)
                if stage == 10 and c == 0:
                    dve.wait_ge(w_out_hi_done, 1)
                    nc.vector.tensor_tensor(w_out_lo[:], w_out_sb[:], w_out_hi[:].bitcast(F32),
                                            ALU.subtract).then_inc(w_out_lo_done, 1)
                    dve.wait_ge(router_hi_done, 1)
                    nc.vector.tensor_tensor(router_hl[:, NEXP:2 * NEXP], router_sb[:],
                                            router_hl[:, 0:NEXP].bitcast(F32),
                                            ALU.subtract).then_inc(router_lo_done, 1)
                if stage == 11:
                    dve.wait_ge(y_mm, c + 1)
                    dve.wait_ge(uc_done[X0], c + 1)
                    if c > 0:
                        dve.wait_ge(gated_lo_done, c)
                    nc.vector.tensor_tensor(gated[:], ps_b[:], uc[X0][:].rearrange("p b t -> p (b t)"),
                                            ALU.mult).then_inc(gated_done, 1)
                if stage == 14:
                    dve.wait_ge(o_mm, c + 1)
                    moments("o", c, lambda j: ps_b[:, j * P:(j + 1) * P])
                if stage == 16:
                    dve.wait_ge(o_n_done, TILES * (c + 1))
                    nc.vector.tensor_tensor(x1[:, c % 2], o_n[:], x_sb[:, c * TILES:(c + 1) * TILES, :],
                                            ALU.add).then_inc(x1_done, 1)
                    dve.wait_ge(x1_done, c + 1)
                    moments("x1", c, lambda j: x1[:, c % 2, j, :])
                if stage == 17:
                    normalise("x1", c, xf, lambda j: x1[:, c % 2, j, :], xf_done)
                if stage == 18:
                    dve.wait_ge(xfT_hi_done, c + 1)
                    nc.vector.tensor_tensor(xfT_lo[:, c % 2], ps_a[:], xfT_hi[:, c % 2].bitcast(F32),
                                            ALU.subtract).then_inc(xfT_lo_done, 1)
                if stage == 19:
                    gates_a(c)
                if stage == 20:
                    gates_b(c)

            def gates_a(c):
                dve.wait_ge(logits_mm, c + 1)
                src = ps_b[:, 0:TILES * 2 * NEXP].rearrange("p (t h e) -> p t h e", t=TILES, h=2)
                rb = cols_sb[:, C_RB:C_RB + NEXP].unsqueeze(1).broadcast_to([P, TILES, NEXP])
                nc.vector.tensor_tensor(lg_a[:], src[:, :, 0, :], rb, ALU.add).then_inc(lg_a_done, 1)
                dve.wait_ge(lg_a_done, c + 1)
                nc.vector.tensor_tensor(lg[:], src[:, :, 1, :], lg_a[:], ALU.add).then_inc(lg_done, 1)
                dve.wait_ge(lg_done, c + 1)
                nc.vector.reduce_max(lg_max[:], lg[:], AX_X).then_inc(lg_max_done, 1)
                dve.wait_ge(lg_max_done, c + 1)
                nc.vector.tensor_tensor(lg_z[:], lg[:], lg_max[:].unsqueeze(2).broadcast_to([P, TILES, NEXP]),
                                        ALU.subtract).then_inc(lg_z_done, 1)

            def gates_b(c):
                full = [P, TILES, NEXP, NEXP]
                dve.wait_ge(ge_done, c + 1)
                other = ge[:].unsqueeze(2).broadcast_to(full)
                own = ge[:].unsqueeze(3).broadcast_to(full)
                flat = "p t i j -> p t (i j)"
                nc.vector.tensor_tensor(beats[:], other, own, ALU.is_gt).then_inc(beats_done, 1)
                nc.vector.tensor_tensor(ties[:], other, own, ALU.is_equal).then_inc(ties_done, 1)
                dve.wait_ge(ties_done, c + 1)
                if c == 0:
                    dve.wait_ge(ld["tri"], 16)
                nc.vector.tensor_tensor(ties_low[:].rearrange(flat), ties[:].rearrange(flat),
                                        tri_sb[:].unsqueeze(1).broadcast_to([P, TILES, NEXP * NEXP]),
                                        ALU.mult).then_inc(ties_low_done, 1)
                dve.wait_ge(beats_done, c + 1)
                dve.wait_ge(ties_low_done, c + 1)
                nc.vector.tensor_tensor(ahead[:], beats[:], ties_low[:], ALU.add).then_inc(ahead_done, 1)
                dve.wait_ge(ahead_done, c + 1)
                nc.vector.reduce_sum(place[:], ahead[:], AX_X).then_inc(place_done, 1)
                dve.wait_ge(place_done, c + 1)
                nc.vector.scalar_tensor_tensor(out=kept[:], in0=place[:], scalar=2.0, in1=ge[:],
                                               op0=ALU.is_lt, op1=ALU.mult).then_inc(kept_done, 1)
                dve.wait_ge(kept_done, c + 1)
                nc.vector.reduce_sum(ksum[:], kept[:], AX_X).then_inc(ksum_done, 1)
                dve.wait_ge(ksum_done, c + 1)
                nc.vector.reciprocal(krec[:], ksum[:]).then_inc(krec_done, 1)
                dve.wait_ge(krec_done, c + 1)
                nc.vector.tensor_tensor(gates[:, c % 2], kept[:],
                                        krec[:].unsqueeze(2).broadcast_to([P, TILES, NEXP]),
                                        ALU.mult).then_inc(gates_done, 1)

            def weigh_expert(n):
                c, e = divmod(n, NEXP)
                dve.wait_ge(et_mm, n + 1)
                src = ps_et[:].rearrange("p (t d) -> p t d", t=TILES)
                gate = gates[:, c % 2, :, e:e + 1].broadcast_to([P, TILES, P])
                if e == 0:
                    dve.wait_ge(gates_done, c + 1)
                    if c > 0:
                        dve.wait_ge(acc_n_done, TILES * c)
                    nc.vector.tensor_tensor(acc[:], src, gate, ALU.mult).then_inc(acc_first, 1)
                else:
                    if 3 * c + e > 1:
                        dve.wait_ge(acc_added, 3 * c + e - 1)
                    nc.vector.tensor_tensor(weighted[:], src, gate, ALU.mult).then_inc(weighted_done, 1)

            for g in range(FIRST, LAST):
                if 0 <= g < NG:
                    dve.wait_ge(silu_done, g + 1)
                    dve.wait_ge(h3_mm, g + 1)
                    if g >= 2:
                        dve.wait_ge(hid_hi_done, g - 1)
                        dve.wait_ge(hid_lo_done, g - 1)
                    nc.vector.tensor_tensor(hid[:, g % 2], ps_h3[g % 2][:], silu[:, g % 2],
                                            ALU.mult).then_inc(hid_done, 1)
                if 0 <= g - 1 < NG:
                    dve.wait_ge(hid_hi_done, g)
                    nc.vector.tensor_tensor(hid_lo[:, (g - 1) % 4], hid[:, (g - 1) % 2],
                                            hid_hi[:, (g - 1) % 4].bitcast(F32),
                                            ALU.subtract).then_inc(hid_lo_done, 1)
                if g >= 7 and (g - 7) % FT == 0 and (g - 7) // FT < NG // FT:
                    weigh_expert((g - 7) // FT)
                if g >= STEPS and (g - 4) % STEPS == 0:
                    cc = g // STEPS - 1
                    dve.wait_ge(acc_added, 3 * (cc + 1))
                    moments("moe", cc, lambda j: acc[:, j, :])
                if g >= STEPS and (g - 5) % STEPS == 0:
                    cc = g // STEPS - 1
                    dve.wait_ge(acc_n_done, TILES * (cc + 1))
                    nc.vector.tensor_tensor(y[:], acc_n[:], x1[:, cc % 2], ALU.add).then_inc(y_done, 1)
                for c, stage in hyena_at(g):
                    hyena(c, stage)


def _split_table(t):
    t = t.astype(np.float32)
    bits = t.view(np.uint32).astype(np.uint64)
    bits = ((bits + 0x7FF + ((bits >> 12) & 1)) & 0xFFFFF000).astype(np.uint32)
    hi = bits.view(np.float32)
    return hi, t - hi


def _transform_tables():
    n = LFILT
    t = np.arange(SEQ, dtype=np.int64)
    even, odd = 2 * np.arange(P), 2 * np.arange(P) + 1

    def turn(f):
        return 2 * np.pi * ((t[:, None] * f[None, :]) % n) / n

    alternate = np.where(t % 2 == 0, 1.0, -1.0)
    forward = [np.cos(turn(even)), -np.sin(turn(even)), np.cos(turn(odd)), -np.sin(turn(odd))]
    forward[1][:, 0] = alternate
    inverse = [2 / n * np.cos(turn(even)).T, -2 / n * np.sin(turn(even)).T,
               2 / n * np.cos(turn(odd)).T, -2 / n * np.sin(turn(odd)).T]
    inverse[0][0] = 1 / n
    inverse[1][0] = alternate / n
    fwd = np.stack(_split_table(np.concatenate(forward, 1).reshape(2, P, LFILT)))
    inv = np.stack(_split_table(np.stack(inverse)))
    return (np.ascontiguousarray(fwd.transpose(2, 0, 1, 3)), np.ascontiguousarray(inv.transpose(2, 0, 1, 3)))


def _filter_tables():
    t = np.linspace(0.0, 1.0, LFILT).astype(np.float32)
    w = (2.0 * np.pi * np.arange(LFILT) / LFILT).astype(np.float32)
    fw = (np.float32(1e-4) * w).astype(np.float64)
    z = np.stack([t, np.cos(fw), -np.sin(fw)]).astype(np.float32)
    deltas = np.linspace(np.log(0.01) / 1.5, np.log(0.01) / 0.3, P)
    window = np.exp(-t[:, None].astype(np.float64) * np.abs(deltas)[None, :]) + 0.05
    return z, window.astype(np.float32)


def kernel(**inputs):
    import concourse.bacc as _bacc
    from concourse.bass_utils import run_bass_kernel_spmd as _run

    d = {k.removeprefix("L0_"): np.asarray(v) for k, v in inputs.items()}
    u = d["attn_u"]
    x = np.ascontiguousarray(u.reshape(-1, P))
    z, window = _filter_tables()
    fwd, inv = _transform_tables()
    half = P // 2

    def twice(v):
        return np.concatenate([v, v])[:, None]

    cols = np.concatenate(
        [d["attn_b_in"].reshape(3, P).T,
         d["attn_sf_w"].reshape(3, P, 3).transpose(1, 0, 2).reshape(P, 9),
         d["attn_sf_b"].reshape(3, P).T,
         *(twice(d[f"attn_f_b{n}"]) for n in (1, 2, 3)),
         *(twice(d[f"attn_freq{n}"]) for n in (1, 2, 3)),
         np.broadcast_to(d["ffn_router_b"], (P, NEXP)), d["attn_b_out"][:, None]], axis=1)
    filt_z = np.zeros((6, P + SEQ), np.float32)
    filt_mats = np.zeros((P, 3, P), np.float32)
    for h in range(2):
        a = slice(h * half, (h + 1) * half)
        filt_z[3 * h:3 * h + 3, a] = d["attn_f_w1"]
        filt_z[3 * h:3 * h + 3, P:] = z[:, h * SEQ:(h + 1) * SEQ]
        filt_mats[a, 0, a] = d["attn_f_w2"]
        filt_mats[a, 1, a] = d["attn_f_w3"]
        filt_mats[a, 2, :] = d["attn_f_wout"]
    arrays = {
        "x": x, "w_in": d["attn_w_in"], "w_out": d["attn_w_out"], "cols": cols, "fbias": d["attn_filt_bias"][None, :],
        "filt_z": filt_z, "filt_mats": filt_mats,
        "decay": np.ascontiguousarray(window.reshape(4, P, P).transpose(1, 0, 2)),
        "router": d["ffn_router_w"], "w1": d["ffn_w1"], "w3": d["ffn_w3"], "w2": d["ffn_w2"],
        "fwd": fwd, "inv": inv, "ident": np.eye(P, dtype=np.float32),
        "tri": np.ascontiguousarray(np.broadcast_to(np.tril(np.ones((NEXP, NEXP), np.float32), -1).reshape(1, -1),
                                                    (P, NEXP * NEXP))),
    }
    nc = _bacc.Bacc("TRN2", target_bir_lowering=False, num_devices=1)
    ins, args = {}, {}
    for name, a in arrays.items():
        a = np.ascontiguousarray(a)
        ins[f"in_{name}"] = a
        args[name] = nc.dram_tensor(f"in_{name}", a.shape, mybir.dt.from_np(a.dtype), kind="ExternalInput").ap()
    out = nc.dram_tensor("out_x", x.shape, F32, kind="ExternalOutput").ap()
    build(nc, out=out, **args)
    got = _run(nc, [ins], core_ids=[0]).results[0]["out_x"]
    return got.reshape(u.shape)
```

```python
from contextlib import ExitStack

import numpy as np

import concourse.bass as bass
from concourse import mybir

F32 = mybir.dt.float32
F32R = mybir.dt.float32r
ALU = mybir.AluOpType
ACT = mybir.ActivationFunctionType
AX_X = mybir.AxisListType.X

P = 128
LFILT = 512
NEXP = 4
HID = 512
FT = HID // P
TILES = 4
CHUNK = TILES * P
SEQ = 256
BPC = CHUNK // SEQ
STEPS = NEXP * FT
EPS = 1e-5
ROUND = 1.5 * 2.0 ** 23
TURN = 6.283185

DOWN = 3
OUT_AT = FT - 1 + DOWN
POOL_LO = (1, 2, 3, 4, 5, 7, 8, 10, 11, 12, 14, 15)
WARM = [
    {"filter layer 2": 4, "x0": 3, "filter taps": 3, "filter transform": 16, "even": 2,
     "inverse": 16, "o proj": 12, "o T": 6, "logits": 8},
    {"filter layer 1": 5, "x1": 5, "v": 2, "v T": 2, "filter transform": 1,
     "odd": 2, "inverse": 5, "o proj": 5, "logits": 3, "experts": 6},
]
PE_AT = {
    "filter layer 0": (20, 2),
    "filter layer 1": (26, 1),
    "xn T": (27, 0),
    "filter layer 2": (27, 2),
    "x1": (28, 1),
    "v": (29, 0),
    "filter taps": (29, 2),
    "x0": (30, 0),
    "filter transform": (30, 2),
    "v T": (31, 1),
    "even": (33, 1),
    "odd": (38, 0),
    "inverse": (40, 0),
    "o proj": (41, 1),
    "o T": (42, 0),
    "xf T": (46, 0),
    "logits": (46, 2),
}
ACT_AT = {
    "filter sin 0": (16, 1),
    "w_in hi": (23, 1),
    "filter sin 1": (23, 1),
    "xnT hi": (27, 0),
    "x1": (28, 2),
    "filter sin 2": (28, 2),
    "v": (29, 0),
    "filter fold hi": (29, 2),
    "x0": (30, 0),
    "split 0": (30, 1),
    "split 1": (30, 2),
    "split 2": (31, 0),
    "vT hi": (31, 2),
    "split 3": (37, 2),
    "filter spectrum": (38, 0),
    "even hi": (38, 0),
    "odd hi": (38, 2),
    "split 4": (39, 0),
    "split 5": (39, 1),
    "w_out hi": (39, 1),
    "gated hi": (39, 2),
    "split 6": (41, 0),
    "split 7": (41, 0),
    "o bias": (41, 0),
    "split 8": (41, 2),
    "o norm": (43, 2),
    "xfT hi": (45, 1),
    "split 9": (46, 2),
    "split 10": (47, 1),
    "split 11": (47, 2),
}
DVE_AT = {
    "x moments": (20, 2),
    "set-up": (21, 0),
    "filter layer 0": (21, 1),
    "x norm": (23, 2),
    "filter layer 1": (23, 2),
    "w_in lo": (26, 0),
    "xnT lo": (26, 2),
    "filter layer 2": (27, 1),
    "x1": (28, 2),
    "filter fold": (29, 2),
    "v": (29, 2),
    "filter fold lo": (30, 0),
    "x0": (30, 1),
    "vT lo": (30, 2),
    "filter spectrum": (31, 0),
    "even": (32, 2),
    "odd": (37, 2),
    "odd sum": (37, 2),
    "even lo": (37, 2),
    "odd lo": (38, 0),
    "gated": (39, 1),
    "w_out lo": (39, 2),
    "gated lo": (39, 2),
    "o moments": (41, 1),
    "o + x": (43, 2),
    "x1 norm": (44, 2),
    "xfT lo": (45, 1),
    "logits": (46, 0),
    "gates": (47, 2),
}
POOL_AT = {
    "x rstd": (21, 2),
    "vx": (30, 0),
    "split 0": (30, 1),
    "split 1": (31, 0),
    "split 2": (31, 0),
    "even sum": (32, 1),
    "split 3": (38, 1),
    "split 4": (40, 1),
    "split 5": (40, 2),
    "split 6": (42, 0),
    "o rstd": (42, 1),
    "x1 rstd": (43, 0),
    "split 7": (43, 1),
    "split 8": (43, 1),
    "exp": (46, 2),
    "split 9": (47, 0),
    "split 10": (47, 2),
    "split 11": (48, 1),
}
PE_AHEAD = {
    "xn T": (26, 0),
    "x1": (29, 1),
    "v": (29, 1),
    "x0": (29, 2),
    "v T": (30, 2),
    "odd": (34, 0),
    "inverse": (39, 1),
}
ACT_AHEAD = {
    "xnT hi": (25, 0),
    "x0": (29, 1),
    "vT hi": (29, 1),
    "even hi": (35, 1),
    "odd hi": (36, 1),
    "gated hi": (39, 1),
    "o norm": (43, 1),
    "xfT hi": (46, 0),
}
DVE_AHEAD = {
    "x moments": (22, 2),
    "xnT lo": (25, 1),
    "x0": (30, 2),
    "even": (32, 0),
    "odd": (34, 2),
    "odd sum": (35, 2),
    "odd lo": (37, 1),
    "gated": (38, 0),
    "o moments": (41, 2),
    "x1 norm": (44, 0),
    "xfT lo": (45, 0),
}
POOL_AHEAD = {
    "x rstd": (23, 2),
    "vx": (27, 1),
    "even sum": (33, 1),
    "o rstd": (41, 1),
    "x1 rstd": (43, 2),
}

C_BIN, C_SFW, C_SFB, C_FB, C_FF, C_RB, C_BOUT, NCOL = 0, 3, 12, 15, 18, 21, 25, 26
X0, X1, V = 0, 1, 2


def build(nc, x, w_in, w_out, cols, fbias, filt_z, filt_mats, decay, router, w1, w3, w2,
          fwd, inv, ident, tri, out):
    ntok = x.shape[0]
    NCH = ntok // CHUNK
    NG = NCH * STEPS

    with ExitStack() as ctx:
        def sb(name, shape, dt=F32):
            return ctx.enter_context(nc.sbuf_tensor(name, shape, dt))

        def ps(name, shape=(P, 512)):
            return ctx.enter_context(nc.psum_tensor(name, list(shape), F32))

        def sem(name):
            return ctx.enter_context(nc.semaphore(name))

        x_sb = sb("x_sb", [P, NCH * TILES, P])
        cols_sb = sb("cols_sb", [P, NCOL])
        fbias_sb = sb("fbias_sb", [1, P])
        filt_z_sb = sb("filt_z_sb", [6, P + SEQ])
        filt_mats_sb = sb("filt_mats_sb", [P, 3, P])
        decay_sb = sb("decay_sb", [P, 4, P])
        ident_sb = sb("ident_sb", [P, P])
        tri_sb = sb("tri_sb", [P, NEXP * NEXP])
        fwd_sb = sb("fwd_sb", [P, 2, 2, LFILT], F32R)
        inv_sb = sb("inv_sb", [P, 2, 4, SEQ], F32R)
        w_in_sb = sb("w_in_sb", [P, 3 * P])
        w_in_hi = sb("w_in_hi", [P, 3 * P], F32R)
        w_in_lo = sb("w_in_lo", [P, 3 * P], F32R)
        w_out_sb = sb("w_out_sb", [P, P])
        w_out_hi = sb("w_out_hi", [P, P], F32R)
        w_out_lo = sb("w_out_lo", [P, P], F32R)
        router_sb = sb("router_sb", [P, NEXP])
        router_hl = sb("router_hl", [P, 2 * NEXP], F32R)
        EW_RING = 6
        ew_sb = [sb(f"ew_sb{i}", [P, HID]) for i in range(EW_RING)]
        ew_hi = [sb(f"ew{n}_hi", [P, NEXP, HID], F32R) for n in (1, 3, 2)]
        ew_lo = [sb(f"ew{n}_lo", [P, NEXP, HID], F32R) for n in (1, 3, 2)]
        tap2_bias = sb("tap2_bias", [P, 3])
        warmed = sb("warmed", [P, 1])
        fturns = sb("fturns", [P, 3])
        minus_half = sb("minus_half", [P, TILES])
        signs = sb("signs", [P, 2])
        e_base = sb("e_base", [P, TILES * NEXP])

        khat_a = sb("khat_a", [P, 4, BPC, P])
        khat_b = sb("khat_b", [P, 4, BPC, P])

        kinds = ("x", "o", "x1", "moe")
        stats = {k: sb(f"stats_{k}", [P, TILES, 6]) for k in kinds}
        mv = {k: sb(f"mv_{k}", [P, TILES, 2]) for k in kinds}
        veps = {k: sb(f"veps_{k}", [P, TILES]) for k in kinds}
        rstd = {k: sb(f"rstd_{k}", [P, TILES]) for k in kinds}
        negm = {k: sb(f"negm_{k}", [P, TILES]) for k in ("o", "moe")}
        nbias = {k: sb(f"nbias_{k}", [P, TILES]) for k in ("o", "moe")}
        xn = sb("xn", [P, TILES, P])
        xnT_hi = sb("xnT_hi", [P, CHUNK], F32R)
        xnT_lo = sb("xnT_lo", [P, CHUNK], F32R)
        up = [sb(f"up{s}", [P, BPC, SEQ + 2]) for s in range(3)]
        tap2 = [sb(f"tap2_{s}", [P, BPC, SEQ]) for s in range(3)]
        uc = tap2
        vx = sb("vx", [P, BPC, SEQ])
        vT_hi = sb("vT_hi", [P, 2, BPC, P], F32R)
        vT_lo = sb("vT_lo", [P, 2, BPC, P], F32R)
        pa = sb("pa", [P, 2, 2, BPC * P])
        pb = sb("pb", [P, 2, 2, BPC * P])
        yh = pa
        yh_hi = sb("yh_hi", [P, 2, 2, BPC * P], F32R)
        yh_lo = sb("yh_lo", [P, 2, 2, BPC * P], F32R)
        gated = sb("gated", [P, CHUNK])
        gated_hi = sb("gated_hi", [P, CHUNK], F32R)
        gated_lo = sb("gated_lo", [P, CHUNK], F32R)
        oT = sb("oT", [P, CHUNK])
        o_n = sb("o_n", [P, TILES, P])
        x1 = sb("x1", [P, 2, TILES, P])
        xf = sb("xf", [P, TILES, P])
        xfT_hi = sb("xfT_hi", [P, 2, CHUNK], F32R)
        xfT_lo = sb("xfT_lo", [P, 2, CHUNK], F32R)

        lg_a = sb("lg_a", [P, TILES, NEXP])
        lg = sb("lg", [P, TILES, NEXP])
        lg_max = sb("lg_max", [P, TILES])
        lg_z = sb("lg_z", [P, TILES, NEXP])
        ge = sb("ge", [P, TILES, NEXP])
        beats = sb("beats", [P, TILES, NEXP, NEXP])
        ties = sb("ties", [P, TILES, NEXP, NEXP])
        ties_low = sb("ties_low", [P, TILES, NEXP, NEXP])
        ahead = sb("ahead", [P, TILES, NEXP, NEXP])
        place = sb("place", [P, TILES, NEXP])
        kept = sb("kept", [P, TILES, NEXP])
        ksum = sb("ksum", [P, TILES])
        krec = sb("krec", [P, TILES])
        gates = sb("gates", [P, 2, TILES, NEXP])

        silu = sb("silu", [P, 2, CHUNK])
        hid = sb("hid", [P, 2, CHUNK])
        hid_hi = sb("hid_hi", [P, 4, CHUNK], F32R)
        hid_lo = sb("hid_lo", [P, 4, CHUNK], F32R)
        fpos, fwhole, fpart, fh = (hid[:, i // 2, (i % 2) * SEQ:(i % 2 + 1) * SEQ] for i in range(4))
        taps = silu[:, 0].rearrange("p (i d) -> p i d", i=4)
        fold, fold_hi, fold_lo = (t.rearrange("p (h n) -> p h n", h=2)
                                  for t in (silu[:, 1], hid_hi[:, 0], hid_lo[:, 0]))
        eoT = sb("eoT", [P, CHUNK])
        acc = sb("acc", [P, TILES, P])
        weighted = sb("weighted", [P, TILES, P])
        acc_n = sb("acc_n", [P, TILES, P])
        y = acc_n

        ps_h1 = [ps("ps_h1a"), ps("ps_h1b")]
        ps_h3 = [ps("ps_h3a"), ps("ps_h3b")]
        ps_eo = ps("ps_eo")
        ps_et = ps("ps_et")
        ps_a = ps("ps_a")
        ps_b = ps("ps_b")

        ld_x = [sem(f"ld_x{c}") for c in range(NCH)]
        ld = {k: sem(f"ld_{k}") for k in ("cols", "fbias", "fz", "fmats", "decay", "ident", "tri",
                                         "w_in", "w_out", "router", "fwd", "inv")}
        ld_ew = [[sem(f"ld_ew{m}_{e}") for e in range(NEXP)] for m in range(3)]
        stored = sem("stored")
        consts_set = sem("consts_set")
        pads_set = sem("pads_set")
        ew_hi_done = sem("ew_hi_done")
        ew_lo_done = sem("ew_lo_done")
        w_in_hi_done = sem("w_in_hi_done")
        w_in_lo_done = sem("w_in_lo_done")
        w_out_hi_done = sem("w_out_hi_done")
        w_out_lo_done = sem("w_out_lo_done")
        tap2_bias_a = sem("tap2_bias_a")
        tap2_bias_done = sem("tap2_bias_done")
        f_mm = sem("f_mm")
        fturns_done = sem("fturns_done")
        f_pos = sem("f_pos")
        f_whole = sem("f_whole")
        f_part = sem("f_part")
        f_sin = sem("f_sin")
        taps_mm = sem("taps_mm")
        taps_done = sem("taps_done")
        fold_done = sem("fold_done")
        fold_hi_done = sem("fold_hi_done")
        fold_lo_done = sem("fold_lo_done")
        khat_mm = sem("khat_mm")
        khat_even_copied = sem("khat_even_copied")
        khat_even_done = sem("khat_even_done")
        khat_odd_done = sem("khat_odd_done")
        ln_stats = {k: sem(f"ln_stats_{k}") for k in kinds}
        ln_mv = {k: sem(f"ln_mv_{k}") for k in kinds}
        ln_veps = {k: sem(f"ln_veps_{k}") for k in kinds}
        ln_rstd = {k: sem(f"ln_rstd_{k}") for k in kinds}
        ln_nbias = {k: sem(f"ln_nbias_{k}") for k in ("o", "moe")}
        xn_done = sem("xn_done")
        xnT_mm = sem("xnT_mm")
        xnT_hi_done = sem("xnT_hi_done")
        xnT_lo_done = sem("xnT_lo_done")
        proj_mm = [sem(f"proj_mm{s}") for s in range(3)]
        up_done = [sem(f"up_done{s}") for s in range(3)]
        tap2_done = [sem(f"tap2_done{s}") for s in range(3)]
        tap1_done = [sem(f"tap1_done{s}") for s in range(3)]
        uc_done = [sem(f"uc_done{s}") for s in range(3)]
        vx_done = sem("vx_done")
        vT_mm = sem("vT_mm")
        vT_hi_done = sem("vT_hi_done")
        vT_lo_done = sem("vT_lo_done")
        fwd_mm = [sem("fwd_mm_even"), sem("fwd_mm_odd")]
        prod_a = [sem("prod_a_even"), sem("prod_a_odd")]
        prod_b = [sem("prod_b_even"), sem("prod_b_odd")]
        yh_done = [sem("yh_done_even"), sem("yh_done_odd")]
        yh_hi_done = [sem("yh_hi_even"), sem("yh_hi_odd")]
        yh_lo_done = [sem("yh_lo_even"), sem("yh_lo_odd")]
        y_mm = sem("y_mm")
        gated_done = sem("gated_done")
        gated_hi_done = sem("gated_hi_done")
        gated_lo_done = sem("gated_lo_done")
        oT_mm = sem("oT_mm")
        oT_done = sem("oT_done")
        o_mm = sem("o_mm")
        o_n_done = sem("o_n_done")
        x1_done = sem("x1_done")
        xf_done = sem("xf_done")
        xfT_mm = sem("xfT_mm")
        xfT_hi_done = sem("xfT_hi_done")
        xfT_lo_done = sem("xfT_lo_done")
        router_hi_done = sem("router_hi_done")
        router_lo_done = sem("router_lo_done")
        logits_mm = sem("logits_mm")
        lg_a_done = sem("lg_a_done")
        lg_done = sem("lg_done")
        lg_max_done = sem("lg_max_done")
        lg_z_done = sem("lg_z_done")
        ge_done = sem("ge_done")
        beats_done = sem("beats_done")
        ties_done = sem("ties_done")
        ties_low_done = sem("ties_low_done")
        ahead_done = sem("ahead_done")
        place_done = sem("place_done")
        kept_done = sem("kept_done")
        ksum_done = sem("ksum_done")
        krec_done = sem("krec_done")
        gates_done = sem("gates_done")
        h1_mm = sem("h1_mm")
        h3_mm = sem("h3_mm")
        silu_done = sem("silu_done")
        hid_done = sem("hid_done")
        hid_hi_done = sem("hid_hi_done")
        hid_lo_done = sem("hid_lo_done")
        hid_lo_pool_done = sem("hid_lo_pool_done")
        eo_mm = sem("eo_mm")
        eoT_done = sem("eoT_done")
        et_mm = sem("et_mm")
        weighted_done = sem("weighted_done")
        acc_first = sem("acc_first")
        acc_added = sem("acc_added")
        acc_n_done = sem("acc_n_done")
        y_done = sem("y_done")
        acc_last = sem("acc_last")
        acc_n_last = sem("acc_n_last")

        block = ctx.enter_context(nc.Block())

        x_dram = x.rearrange("(t p) d -> p t d", p=P)
        out_dram = out.rearrange("(t p) d -> p t d", p=P)
        ew_dram = [w1.rearrange("e d f -> d e f"), w3.rearrange("e d f -> d e f"),
                   w2.rearrange("e (j f) d -> f e j d", f=P)]

        FIRST, LAST = -3 * STEPS, NG - FT + OUT_AT + 5

        def expert_at(g, after):
            n, rest = divmod(g - OUT_AT - after, FT)
            return n if rest == 0 and 0 <= n < NG // FT else None

        def chunk_at(g, after):
            n = expert_at(g, after)
            return n // NEXP if n is not None and n % NEXP == NEXP - 1 else None

        LAST_HALVES = slice(TILES // 2, TILES), slice(0, TILES // 2)

        def by_pool(g):
            return g % STEPS in POOL_LO and g < NG - STEPS

        def lo_steps(g, pool):
            return sum(by_pool(i) == pool for i in range(g + 1))

        def due(table, ahead, g, place):
            for c in range(NCH):
                for stage, at in {**table, **(ahead if c == 1 else {})}.items():
                    if at == (g - STEPS * (c - 3), place):
                        yield c, stage

        def wait_lo(engine, g):
            if by_pool(g):
                engine.wait_ge(hid_lo_pool_done, lo_steps(g, True))
            else:
                engine.wait_ge(hid_lo_done, lo_steps(g, False))

        def light_stage(engine, unit, c, stage):
            if stage == "vx":
                engine.wait_ge(uc_done[X1], c + 1)
                engine.wait_ge(uc_done[V], c + 1)
                if c > 0:
                    engine.wait_ge(vT_mm, c)
                unit.tensor_tensor(vx[:], uc[V][:], uc[X1][:], ALU.mult).then_inc(vx_done, 1)
            if stage in ("even sum", "odd sum"):
                h = 0 if stage == "even sum" else 1
                engine.wait_ge(prod_a[h], c + 1)
                engine.wait_ge(prod_b[h], c + 1)
                unit.tensor_tensor(yh[:, h], pa[:, h], pb[:, h], ALU.add).then_inc(yh_done[h], 1)
            if stage in ("even lo", "odd lo"):
                h = 0 if stage == "even lo" else 1
                engine.wait_ge(yh_hi_done[h], c + 1)
                unit.tensor_tensor(yh_lo[:, h], yh[:, h], yh_hi[:, h].bitcast(F32),
                                   ALU.subtract).then_inc(yh_lo_done[h], 1)
            if stage == "gated lo":
                engine.wait_ge(gated_hi_done, c + 1)
                unit.tensor_tensor(gated_lo[:], gated[:], gated_hi[:].bitcast(F32),
                                   ALU.subtract).then_inc(gated_lo_done, 1)

        @block.sync
        def _(sp):
            sp.dma_start(x_sb[:, 0:TILES, :], x_dram[:, 0:TILES, :]).then_inc(ld_x[0], 16)
            sp.dma_start(w_in_sb[:], w_in).then_inc(ld["w_in"], 16)
            sp.dma_start(ident_sb[:], ident).then_inc(ld["ident"], 16)
            sp.dma_start(filt_mats_sb[:], filt_mats).then_inc(ld["fmats"], 16)
            sp.dma_start(decay_sb[:], decay).then_inc(ld["decay"], 16)
            sp.dma_start(fbias_sb[:], fbias).then_inc(ld["fbias"], 16)
            for e in range(NEXP):
                for m in range(3):
                    i = 3 * e + m
                    dst = ew_sb[i % EW_RING][:]
                    src = ew_dram[m][:, e]
                    if i >= EW_RING:
                        sp.wait_ge(ew_lo_done, i - EW_RING + 1)
                    if m == 2:
                        dst = dst.rearrange("p (j d) -> p j d", j=FT)
                    sp.dma_start(dst, src).then_inc(ld_ew[m][e], 16)
                if e == 0:
                    sp.dma_start(w_out_sb[:], w_out).then_inc(ld["w_out"], 16)
                    sp.dma_start(router_sb[:], router).then_inc(ld["router"], 16)
                    sp.dma_start(tri_sb[:], tri).then_inc(ld["tri"], 16)
                if e + 1 < NCH:
                    c = e + 1
                    sp.dma_start(x_sb[:, c * TILES:(c + 1) * TILES, :],
                                 x_dram[:, c * TILES:(c + 1) * TILES, :]).then_inc(ld_x[c], 16)
            for c in range(NCH - 1):
                sp.wait_ge(y_done, c + 1)
                sp.dma_start(out_dram[:, c * TILES:(c + 1) * TILES, :], y[:]).then_inc(stored, 16)
            for i, t in enumerate(LAST_HALVES):
                sp.wait_ge(y_done, NCH + i)
                sp.dma_start(out_dram[:, (NCH - 1) * TILES + t.start:(NCH - 1) * TILES + t.stop, :],
                             y[:, t]).then_inc(stored, 16)
            sp.wait_ge(stored, 16 * (NCH + 1))

        @block.gpsimd
        def _(pool):
            nc.gpsimd.memset(minus_half[:], -0.5).then_inc(consts_set, 1)
            nc.gpsimd.memset(e_base[:], float(np.exp(1.0))).then_inc(consts_set, 1)
            nc.gpsimd.memset(signs[:, 0:1], -1.0).then_inc(consts_set, 1)
            nc.gpsimd.memset(signs[:, 1:2], 1.0).then_inc(consts_set, 1)
            pool.wait_ge(consts_set, 4)
            nc.gpsimd.memset(signs[0:1, :], 0.0).then_inc(consts_set, 1)
            for s in range(3):
                nc.gpsimd.memset(up[s][:, :, 0:2], 0.0).then_inc(pads_set, 1)

            def inv_std(kind, c):
                pool.wait_ge(ln_veps[kind], (2 if kind in negm else 1) * (c + 1))
                if c == 0:
                    pool.wait_ge(consts_set, 2)
                nc.gpsimd.tensor_tensor(rstd[kind][:], veps[kind][:], minus_half[:],
                                        ALU.pow).then_inc(ln_rstd[kind], 1)
                pool.wait_ge(ln_rstd[kind], c + 1)
                if kind in negm:
                    nc.gpsimd.tensor_tensor(nbias[kind][:], negm[kind][:], rstd[kind][:],
                                            ALU.mult).then_inc(ln_nbias[kind], 1)

            def split_matrix(i):
                e, m = divmod(i, 3)
                pool.wait_ge(ew_hi_done, i + 1)
                nc.gpsimd.tensor_tensor(ew_lo[m][:, e, :], ew_sb[i % EW_RING][:],
                                        ew_hi[m][:, e, :].bitcast(F32), ALU.subtract).then_inc(ew_lo_done, 1)

            def hyena(c, stage):
                if stage == "x rstd":
                    inv_std("x", c)
                    if c == 0:
                        pool.dma_start(fwd_sb[:], fwd).then_inc(ld["fwd"], 16)
                        pool.dma_start(inv_sb[:], inv).then_inc(ld["inv"], 16)
                if stage.startswith("split") and c == 0:
                    split_matrix(int(stage.split()[1]))
                light_stage(pool, nc.gpsimd, c, stage)
                if stage == "o rstd":
                    inv_std("o", c)
                if stage == "x1 rstd":
                    inv_std("x1", c)
                if stage == "exp":
                    pool.wait_ge(lg_z_done, c + 1)
                    nc.gpsimd.tensor_tensor(ge[:], e_base[:].rearrange("p (t e) -> p t e", e=NEXP),
                                            lg_z[:], ALU.pow).then_inc(ge_done, 1)

            for g in range(FIRST, LAST):
                if 0 <= g - 1 < NG and by_pool(g - 1):
                    pool.wait_ge(hid_hi_done, g)
                    nc.gpsimd.tensor_tensor(hid_lo[:, (g - 1) % 4], hid[:, (g - 1) % 2],
                                            hid_hi[:, (g - 1) % 4].bitcast(F32),
                                            ALU.subtract).then_inc(hid_lo_pool_done, 1)
                n = expert_at(g, 2)
                if n is not None:
                    c, e = divmod(n, NEXP)
                    if e > 0 and n < NG // FT - 1:
                        added = 3 * c + e
                        pool.wait_ge(weighted_done, added)
                        pool.wait_ge(acc_first, c + 1)
                        if e > 1:
                            pool.wait_ge(acc_added, added - 1)
                        nc.gpsimd.tensor_tensor(acc[:], acc[:], weighted[:], ALU.add).then_inc(acc_added, 1)
                if chunk_at(g, 3) is not None:
                    inv_std("moe", chunk_at(g, 3))
                for place in range(3):
                    for c, stage in due(POOL_AT, POOL_AHEAD, g, place):
                        hyena(c, stage)

        @block.tensor
        def _(pe):
            def product(dst, a_hi, a_lo, b_hi, b_lo, start=True, stop=True):
                nc.tensor.matmul(dst, a_hi, b_hi, start=start, stop=False)
                nc.tensor.matmul(dst, a_lo, b_hi, start=False, stop=False)
                return nc.tensor.matmul(dst, a_hi, b_lo, start=False, stop=stop)

            def transposes(dst, tile_of, tile_done=None, c=0):
                for j in range(TILES):
                    if tile_done is not None:
                        pe.wait_ge(tile_done, TILES * c + j + 1)
                    last = nc.tensor.transpose(dst[:, j * P:(j + 1) * P], tile_of(j), ident_sb[:])
                return last

            def projection(c, s, bank):
                for n in range(3):
                    a = (w_in_hi, w_in_lo, w_in_hi)[n][:, s * P:(s + 1) * P]
                    b = (xnT_hi, xnT_hi, xnT_lo)[n][:]
                    if n == 2:
                        pe.wait_ge(xnT_lo_done, c + 1)
                    last = nc.tensor.matmul(bank[:], a, b, start=(n == 0), stop=(n == 2))
                last.then_inc(proj_mm[s], 1)

            def transform(c, half, bank):
                for i in range(2):
                    f0 = (2 * half + i) * P
                    for kt in range(2):
                        last = product(bank[:, i * BPC * P:(i + 1) * BPC * P],
                                       fwd_sb[:, 0, kt, f0:f0 + P], fwd_sb[:, 1, kt, f0:f0 + P],
                                       vT_hi[:, kt].rearrange("p b d -> p (b d)"),
                                       vT_lo[:, kt].rearrange("p b d -> p (b d)"),
                                       start=(kt == 0), stop=(kt == 1))
                last.then_inc(fwd_mm[half], 1)

            def filter_layer(n):
                bank = (ps_h1[0], ps_h1[1], ps_h3[0])[n]
                if n == 0:
                    pe.wait_ge(ld["fz"], 16)
                    last = nc.tensor.matmul(bank[:, 0:SEQ], filt_z_sb[:, 0:P], filt_z_sb[:, P:P + SEQ],
                                            start=True, stop=True)
                else:
                    if n == 1:
                        pe.wait_ge(ld["fmats"], 16)
                    pe.wait_ge(f_sin, n)
                    last = nc.tensor.matmul(bank[:, 0:SEQ], filt_mats_sb[:, n - 1, :], fh,
                                            start=True, stop=True)
                last.then_inc(f_mm, 1)

            def filter_taps():
                pe.wait_ge(f_sin, 3)
                half = P // 2
                for i in range(4):
                    h = i // 2
                    bank = (ps_h3[1], ps_et)[h]
                    last = nc.tensor.matmul(bank[:, (i % 2) * P:(i % 2 + 1) * P],
                                            fh[h * half:(h + 1) * half, (i % 2) * P:(i % 2 + 1) * P],
                                            filt_mats_sb[h * half:(h + 1) * half, 2, :],
                                            start=True, stop=True)
                    if i % 2:
                        last.then_inc(taps_mm, 1)

            def filter_transform():
                pe.wait_ge(ld["fwd"], 16)
                pe.wait_ge(fold_hi_done, 1)
                pe.wait_ge(fold_lo_done, 1)
                for i in range(4):
                    bank = (ps_eo, ps_et)[i // 2]
                    for kt in range(2):
                        last = product(bank[:, (i % 2) * P:(i % 2 + 1) * P],
                                       fwd_sb[:, 0, kt, i * P:(i + 1) * P],
                                       fwd_sb[:, 1, kt, i * P:(i + 1) * P],
                                       fold_hi[:, i // 2, kt * P:(kt + 1) * P],
                                       fold_lo[:, i // 2, kt * P:(kt + 1) * P],
                                       start=(kt == 0), stop=(kt == 1))
                    if i % 2:
                        last.then_inc(khat_mm, 1)

            bank_of = {stage: bank for bank, stages in
                       (("a", ("xn T", "v", "v T", "odd", "o proj", "xf T")),
                        ("b", ("x1", "x0", "even", "inverse", "o T", "logits"))) for stage in stages}
            last_in = {}

            def wait_for_bank(c, stage):
                bank = bank_of[stage]
                before, chunk = last_in.get(bank, (None, 0))
                last_in[bank] = stage, c
                if before == "xn T":
                    pe.wait_ge(xnT_lo_done, chunk + 1)
                if before in ("x1", "v", "x0"):
                    s = {"x1": X1, "v": V, "x0": X0}[before]
                    pe.wait_ge(up_done[s], chunk + 1)
                    pe.wait_ge(tap2_done[s], chunk + 1)
                if before == "v T":
                    pe.wait_ge(vT_lo_done, chunk + 1)
                if before in ("even", "odd"):
                    h = 0 if before == "even" else 1
                    pe.wait_ge(prod_a[h], chunk + 1)
                    pe.wait_ge(prod_b[h], chunk + 1)
                if before == "inverse":
                    pe.wait_ge(gated_done, chunk + 1)
                if before == "o proj":
                    pe.wait_ge(oT_done, chunk + 1)
                if before == "o T":
                    pe.wait_ge(o_n_done, TILES * (chunk + 1))
                if before == "xf T":
                    pe.wait_ge(xfT_lo_done, chunk + 1)
                if before == "logits":
                    pe.wait_ge(lg_done, chunk + 1)

            def keep_clock(products):
                if products > 0:
                    pe.wait_ge(w_in_hi_done, 1)
                    pe.wait_ge(f_pos, 1)
                for _ in range(products):
                    nc.tensor.matmul(ps_h1[0][:, 0:3 * P], w_in_hi[:, 0:P], w_in_hi[:], start=True, stop=True)

            def hyena(c, stage):
                if stage in bank_of:
                    wait_for_bank(c, stage)
                if stage.startswith("filter layer") and c == 0:
                    filter_layer(int(stage[-1]))
                if stage == "filter taps" and c == 0:
                    filter_taps()
                if stage == "filter transform" and c == 0:
                    filter_transform()
                if stage == "xn T":
                    if c == 0:
                        pe.wait_ge(ld["ident"], 16)
                    transposes(ps_a, lambda j: xn[:, j, :], xn_done, c).then_inc(xnT_mm, 1)
                if stage == "x1":
                    if c == 0:
                        pe.wait_ge(w_in_hi_done, 1)
                        pe.wait_ge(w_in_lo_done, 1)
                    pe.wait_ge(xnT_hi_done, c + 1)
                    projection(c, X1, ps_b)
                if stage == "v":
                    projection(c, V, ps_a)
                if stage == "x0":
                    projection(c, X0, ps_b)
                if stage == "v T":
                    pe.wait_ge(vx_done, c + 1)
                    for kt in range(2):
                        for b in range(BPC):
                            at = (kt * BPC + b) * P
                            last = nc.tensor.transpose(ps_a[:, at:at + P], vx[:, b, kt * P:(kt + 1) * P],
                                                       ident_sb[:])
                    last.then_inc(vT_mm, 1)
                if stage == "even":
                    if c == 0:
                        pe.wait_ge(ld["fwd"], 16)
                    pe.wait_ge(vT_hi_done, c + 1)
                    pe.wait_ge(vT_lo_done, c + 1)
                    transform(c, 0, ps_b)
                if stage == "odd":
                    pe.wait_ge(vT_hi_done, c + 1)
                    pe.wait_ge(vT_lo_done, c + 1)
                    transform(c, 1, ps_a)
                if stage == "inverse":
                    if c == 0:
                        pe.wait_ge(ld["inv"], 16)
                    for b in range(BPC):
                        for i in range(4):
                            h = i // 2
                            if b == 0 and i % 2 == 0:
                                pe.wait_ge(yh_hi_done[h], c + 1)
                                pe.wait_ge(yh_lo_done[h], c + 1)
                            hi = yh_hi[:, h, i % 2, b * P:(b + 1) * P]
                            lo = yh_lo[:, h, i % 2, b * P:(b + 1) * P]
                            last = product(ps_b[:, b * SEQ:(b + 1) * SEQ], hi, lo,
                                           inv_sb[:, 0, i, :], inv_sb[:, 1, i, :],
                                           start=(i == 0), stop=(i == 3))
                    last.then_inc(y_mm, 1)
                if stage == "o proj":
                    if c == 0:
                        pe.wait_ge(w_out_hi_done, 1)
                        pe.wait_ge(w_out_lo_done, 1)
                    pe.wait_ge(gated_hi_done, c + 1)
                    pe.wait_ge(gated_lo_done, c + 1)
                    product(ps_a[:], w_out_hi[:], w_out_lo[:], gated_hi[:], gated_lo[:]).then_inc(oT_mm, 1)
                if stage == "o T":
                    pe.wait_ge(oT_done, c + 1)
                    transposes(ps_b, lambda j: oT[:, j * P:(j + 1) * P]).then_inc(o_mm, 1)
                if stage == "xf T":
                    transposes(ps_a, lambda j: xf[:, j, :], xf_done, c).then_inc(xfT_mm, 1)
                if stage == "logits":
                    if c == 0:
                        pe.wait_ge(router_hi_done, 1)
                        pe.wait_ge(router_lo_done, 1)
                    pe.wait_ge(xfT_hi_done, c + 1)
                    pe.wait_ge(xfT_lo_done, c + 1)
                    for j in range(TILES):
                        t = slice(j * P, (j + 1) * P)
                        dst = ps_b[:, j * 2 * NEXP:(j + 1) * 2 * NEXP]
                        nc.tensor.matmul(dst, xfT_hi[:, c % 2, t], router_hl[:], start=True, stop=False)
                        last = nc.tensor.matmul(dst, xfT_lo[:, c % 2, t], router_hl[:], start=False, stop=True)
                    last.then_inc(logits_mm, 1)

            def up_product(g, m):
                c, k = divmod(g, STEPS)
                e, f = divmod(k, FT)
                if k == 0:
                    pe.wait_ge(xfT_hi_done, c + 1)
                    pe.wait_ge(xfT_lo_done, c + 1)
                if c == 0 and f == 0:
                    pe.wait_ge(ew_lo_done, 3 * e + 2)
                fs = slice(f * P, (f + 1) * P)
                if g >= 2:
                    pe.wait_ge((silu_done, hid_done)[m], g - 1)
                product((ps_h1, ps_h3)[m][g % 2][:], ew_hi[m][:, e, fs], ew_lo[m][:, e, fs],
                        xfT_hi[:, c % 2], xfT_lo[:, c % 2]).then_inc((h1_mm, h3_mm)[m], 1)

            def down_product(g):
                c, k = divmod(g, STEPS)
                e, f = divmod(k, FT)
                if c == 0 and f == 0:
                    pe.wait_ge(ew_lo_done, 3 * e + 3)
                if f == 0 and g > 0:
                    pe.wait_ge(eoT_done, g // FT)
                pe.wait_ge(hid_hi_done, g + 1)
                wait_lo(pe, g)
                fs = slice(f * P, (f + 1) * P)
                product(ps_eo[:], ew_hi[2][:, e, fs], ew_lo[2][:, e, fs], hid_hi[:, g % 4], hid_lo[:, g % 4],
                        start=(f == 0), stop=(f == FT - 1)).then_inc(eo_mm, 1)

            for g in range(FIRST, LAST):
                if g == 0:
                    keep_clock(WARM[0].get("experts", 0))
                if 0 <= g < NG:
                    up_product(g, 0)
                for c, stage in due(PE_AT, PE_AHEAD, g, 0):
                    if g < 0 and c < 2:
                        keep_clock(WARM[c].get(stage, 0))
                    hyena(c, stage)
                if 0 <= g < NG:
                    up_product(g, 1)
                for c, stage in due(PE_AT, PE_AHEAD, g, 1):
                    if g < 0 and c < 2:
                        keep_clock(WARM[c].get(stage, 0))
                    hyena(c, stage)
                if 0 <= g - DOWN < NG:
                    down_product(g - DOWN)
                n = expert_at(g, 1)
                if n is not None:
                    pe.wait_ge(eoT_done, n + 1)
                    if n > 0:
                        last_c, last_e = divmod(n - 1, NEXP)
                        if last_e == 0:
                            pe.wait_ge(acc_first, last_c + 1)
                        else:
                            pe.wait_ge(weighted_done, 3 * last_c + last_e)
                    transposes(ps_et, lambda j: eoT[:, j * P:(j + 1) * P]).then_inc(et_mm, 1)
                for c, stage in due(PE_AT, PE_AHEAD, g, 2):
                    if g < 0 and c < 2:
                        keep_clock(WARM[c].get(stage, 0))
                    hyena(c, stage)

        @block.scalar
        def _(act):
            act.dma_start(filt_z_sb[:], filt_z).then_inc(ld["fz"], 16)
            act.dma_start(cols_sb[:], cols).then_inc(ld["cols"], 16)

            act.wait_ge(consts_set, 2)
            nc.scalar.activation(warmed[:], minus_half[:, 0:1], ACT.Silu)

            def filter_sin(n):
                act.wait_ge(f_part, n + 1)
                nc.scalar.activation(fh, fpart, ACT.Sin, scale=TURN).then_inc(f_sin, 1)

            def split_matrix(i):
                e, m = divmod(i, 3)
                act.wait_ge(ld_ew[m][e], 16)
                nc.scalar.activation(ew_hi[m][:, e, :], ew_sb[i % EW_RING][:], ACT.Copy).then_inc(ew_hi_done, 1)

            def khat_even():
                act.wait_ge(khat_mm, 1)

                def times(i, n):
                    return ps_eo[:, i * P:(i + 1) * P].unsqueeze(1).broadcast_to([P, n, P])
                nc.scalar.activation(khat_a[:, 0:2].rearrange("p i b d -> p (i b) d"), times(0, 2 * BPC),
                                     ACT.Copy).then_inc(khat_even_copied, 1)
                act.wait_ge(khat_even_copied, 1)
                nc.scalar.activation(khat_a[0:1, 1], times(1, BPC)[0:1], ACT.Copy).then_inc(khat_even_done, 1)
                act.wait_ge(consts_set, 5)
                for i in range(2):
                    nc.scalar.activation(khat_b[:, i], times(1, BPC), ACT.Copy,
                                         scale=signs[:, i:i + 1]).then_inc(khat_even_done, 1)

            def up_and_tap2(c, s, bank):
                act.wait_ge(proj_mm[s], c + 1)
                src = bank[:].rearrange("p (b t) -> p b t", b=BPC)
                if c > 0:
                    act.wait_ge(uc_done[s], c)
                    act.wait_ge(gated_done if s == X0 else vx_done, c)
                nc.scalar.activation(up[s][:, :, 2:], src, ACT.Identity,
                                     bias=cols_sb[:, C_BIN + s:C_BIN + s + 1]).then_inc(up_done[s], 1)
                nc.scalar.activation(tap2[s][:], src, ACT.Identity,
                                     scale=cols_sb[:, C_SFW + 3 * s + 2:C_SFW + 3 * s + 3],
                                     bias=tap2_bias[:, s:s + 1]).then_inc(tap2_done[s], 1)

            def normed(kind, c, dst, src, done, tiles=range(TILES)):
                act.wait_ge(ln_nbias[kind], c + 1)
                for j in tiles:
                    nc.scalar.activation(dst[:, j, :], src(j), ACT.Identity, bias=nbias[kind][:, j:j + 1],
                                         scale=rstd[kind][:, j:j + 1]).then_inc(done, 1)

            def hyena(c, stage):
                if stage.startswith("filter sin") and c == 0:
                    filter_sin(int(stage[-1]))
                if stage.startswith("split") and c == 0:
                    split_matrix(int(stage.split()[1]))
                if stage == "w_in hi" and c == 0:
                    act.wait_ge(ld["w_in"], 16)
                    nc.scalar.activation(w_in_hi[:], w_in_sb[:], ACT.Copy).then_inc(w_in_hi_done, 1)
                if stage == "xnT hi":
                    act.wait_ge(xnT_mm, c + 1)
                    if c > 0:
                        for s in range(3):
                            act.wait_ge(proj_mm[s], c)
                    nc.scalar.activation(xnT_hi[:], ps_a[:], ACT.Copy).then_inc(xnT_hi_done, 1)
                if stage == "x1":
                    if c == 0:
                        act.wait_ge(tap2_bias_done, 1)
                        act.wait_ge(pads_set, 3)
                    up_and_tap2(c, X1, ps_b)
                if stage == "v":
                    up_and_tap2(c, V, ps_a)
                if stage == "x0":
                    up_and_tap2(c, X0, ps_b)
                if stage == "filter spectrum" and c == 0:
                    khat_even()
                if stage == "filter fold hi" and c == 0:
                    act.wait_ge(fold_done, 2)
                    nc.scalar.activation(fold_hi, fold, ACT.Copy).then_inc(fold_hi_done, 1)
                if stage == "vT hi":
                    act.wait_ge(vT_mm, c + 1)
                    if c > 0:
                        act.wait_ge(fwd_mm[1], c)
                    nc.scalar.activation(vT_hi[:].rearrange("p k b d -> p (k b d)"), ps_a[:],
                                         ACT.Copy).then_inc(vT_hi_done, 1)
                if stage in ("even hi", "odd hi"):
                    h = ("even hi", "odd hi").index(stage)
                    act.wait_ge(yh_done[h], c + 1)
                    if c > 0:
                        act.wait_ge(y_mm, c)
                    nc.scalar.activation(yh_hi[:, h], yh[:, h], ACT.Copy).then_inc(yh_hi_done[h], 1)
                if stage == "w_out hi" and c == 0:
                    act.wait_ge(ld["w_out"], 16)
                    nc.scalar.activation(w_out_hi[:], w_out_sb[:], ACT.Copy).then_inc(w_out_hi_done, 1)
                    act.wait_ge(ld["router"], 16)
                    nc.scalar.activation(router_hl[:, 0:NEXP], router_sb[:], ACT.Copy).then_inc(router_hi_done, 1)
                if stage == "gated hi":
                    act.wait_ge(gated_done, c + 1)
                    if c > 0:
                        act.wait_ge(oT_mm, c)
                    nc.scalar.activation(gated_hi[:], gated[:], ACT.Copy).then_inc(gated_hi_done, 1)
                if stage == "o bias":
                    act.wait_ge(oT_mm, c + 1)
                    if c > 0:
                        act.wait_ge(o_mm, c)
                    nc.scalar.activation(oT[:], ps_a[:], ACT.Identity,
                                         bias=cols_sb[:, C_BOUT:C_BOUT + 1]).then_inc(oT_done, 1)
                if stage == "o norm":
                    if c > 0:
                        act.wait_ge(x1_done, 2 * c)
                    normed("o", c, o_n, lambda j: ps_b[:, j * P:(j + 1) * P], o_n_done)
                if stage == "xfT hi":
                    act.wait_ge(xfT_mm, c + 1)
                    if c > 1:
                        act.wait_ge(h3_mm, STEPS * (c - 1))
                    nc.scalar.activation(xfT_hi[:, c % 2], ps_a[:], ACT.Copy).then_inc(xfT_hi_done, 1)

            for g in range(FIRST, LAST):
                if 0 <= g < NG:
                    act.wait_ge(h1_mm, g + 1)
                    if g >= 2:
                        act.wait_ge(hid_done, g - 1)
                    nc.scalar.activation(silu[:, g % 2], ps_h1[g % 2][:], ACT.Silu).then_inc(silu_done, 1)
                for c, stage in due(ACT_AT, ACT_AHEAD, g, 0):
                    hyena(c, stage)
                if 0 <= g - 1 < NG:
                    act.wait_ge(hid_done, g)
                    nc.scalar.activation(hid_hi[:, (g - 1) % 4], hid[:, (g - 1) % 2],
                                         ACT.Copy).then_inc(hid_hi_done, 1)
                for c, stage in due(ACT_AT, ACT_AHEAD, g, 1):
                    hyena(c, stage)
                n = expert_at(g, 0)
                if n is not None:
                    act.wait_ge(eo_mm, FT * (n + 1))
                    if n > 0:
                        act.wait_ge(et_mm, n)
                    nc.scalar.activation(eoT[:], ps_eo[:], ACT.Copy).then_inc(eoT_done, 1)
                cc = chunk_at(g, 4)
                if cc is not None:
                    if cc > 0:
                        act.wait_ge(stored, 16 * cc)
                    normed("moe", cc, acc_n, lambda j: acc[:, j, :], acc_n_done,
                           range(TILES) if cc < NCH - 1 else range(TILES)[LAST_HALVES[1]])
                for c, stage in due(ACT_AT, ACT_AHEAD, g, 2):
                    hyena(c, stage)

        @block.vector
        def _(dve):
            def tile_stats(kind, c, tiles, src):
                if c > 0:
                    dve.wait_ge(*{"x": (xn_done, TILES * c), "o": (o_n_done, TILES * c),
                                  "x1": (xf_done, TILES * c), "moe": (acc_n_done, TILES * c)}[kind])
                for j in tiles:
                    nc.vector.bn_stats(stats[kind][:, j, :], src(j)).then_inc(ln_stats[kind], 1)

            def tile_moments(kind, c):
                for j in range(TILES):
                    dve.wait_ge(ln_stats[kind], TILES * c + j + 1)
                    nc.vector.bn_aggr(mv[kind][:, j, :], stats[kind][:, j, :]).then_inc(ln_mv[kind], 1)
                dve.wait_ge(ln_mv[kind], TILES * (c + 1))
                nc.vector.tensor_scalar(veps[kind][:], mv[kind][:, :, 1], EPS, None,
                                        ALU.add).then_inc(ln_veps[kind], 1)
                if kind in negm:
                    nc.vector.tensor_scalar(negm[kind][:], mv[kind][:, :, 0], -1.0, None,
                                            ALU.mult).then_inc(ln_veps[kind], 1)

            def moments(kind, c, src):
                tile_stats(kind, c, range(TILES), src)
                tile_moments(kind, c)

            def filter_reduce(n):
                bank = (ps_h1[0], ps_h1[1], ps_h3[0])[n]
                dve.wait_ge(f_mm, n + 1)
                nc.vector.tensor_scalar(fpos, bank[:, 0:SEQ], cols_sb[:, C_FB + n:C_FB + n + 1],
                                        fturns[:, n:n + 1], ALU.add, ALU.mult).then_inc(f_pos, 1)
                dve.wait_ge(f_pos, n + 1)
                nc.vector.tensor_scalar(fwhole, fpos, ROUND, ROUND, ALU.add, ALU.subtract).then_inc(f_whole, 1)
                dve.wait_ge(f_whole, n + 1)
                if n > 0:
                    dve.wait_ge(f_sin, n)
                nc.vector.tensor_tensor(fpart, fpos, fwhole, ALU.subtract).then_inc(f_part, 1)

            def normalise(kind, c, dst, src, done, tiles=range(TILES)):
                dve.wait_ge(ln_rstd[kind], c + 1)
                if c > 0:
                    dve.wait_ge(*{"x": (xnT_mm, c), "x1": (xfT_mm, c), "moe": (stored, 16 * c)}[kind])
                for j in tiles:
                    nc.vector.tensor_scalar(dst[:, j, :], src(j), mv[kind][:, j, 0:1], rstd[kind][:, j:j + 1],
                                            ALU.subtract, ALU.mult).then_inc(done, 1)

            def filter_fold():
                dve.wait_ge(taps_mm, 2)
                dve.wait_ge(ld["decay"], 16)
                for h, bank in enumerate((ps_h3[1], ps_et)):
                    nc.vector.tensor_tensor(taps[:, 2 * h:2 * h + 2].rearrange("p i d -> p (i d)"), bank[:, 0:2 * P],
                                            decay_sb[:, 2 * h:2 * h + 2].rearrange("p i d -> p (i d)"),
                                            ALU.mult).then_inc(taps_done, 1)
                dve.wait_ge(taps_done, 2)
                dve.wait_ge(ld["fbias"], 16)
                nc.vector.tensor_tensor(taps[0:1, 0, :], taps[0:1, 0, :], fbias_sb[:],
                                        ALU.add).then_inc(taps_done, 1)
                dve.wait_ge(taps_done, 3)
                for h, op in enumerate((ALU.add, ALU.subtract)):
                    nc.vector.tensor_tensor(fold[:, h], taps[:, 0:2].rearrange("p i d -> p (i d)"),
                                            taps[:, 2:4].rearrange("p i d -> p (i d)"), op).then_inc(fold_done, 1)
            def filter_fold_lo():
                dve.wait_ge(fold_hi_done, 1)
                nc.vector.tensor_tensor(fold_lo, fold, fold_hi.bitcast(F32),
                                        ALU.subtract).then_inc(fold_lo_done, 1)

            def short_conv(c, s):
                src = up[s]
                dve.wait_ge(up_done[s], c + 1)
                dve.wait_ge(tap2_done[s], c + 1)
                nc.vector.scalar_tensor_tensor(out=uc[s][:], in0=src[:, :, 1:SEQ + 1],
                                               scalar=cols_sb[:, C_SFW + 3 * s + 1:C_SFW + 3 * s + 2],
                                               in1=tap2[s][:], op0=ALU.mult, op1=ALU.add).then_inc(tap1_done[s], 1)
                dve.wait_ge(tap1_done[s], c + 1)
                nc.vector.scalar_tensor_tensor(out=uc[s][:], in0=src[:, :, 0:SEQ],
                                               scalar=cols_sb[:, C_SFW + 3 * s:C_SFW + 3 * s + 1],
                                               in1=uc[s][:], op0=ALU.mult, op1=ALU.add).then_inc(uc_done[s], 1)

            def spectrum_product(c, h, bank):
                dve.wait_ge(fwd_mm[h], c + 1)
                if c > 0:
                    dve.wait_ge(yh_lo_done[h], c)
                src = bank[:].rearrange("p (i n) -> p i n", i=2)
                ka = khat_a[:, 2 * h:2 * h + 2].rearrange("p i b d -> p i (b d)")
                kb = khat_b[:, 2 * h:2 * h + 2].rearrange("p i b d -> p i (b d)")
                nc.vector.tensor_tensor(pa[:, h], src, ka, ALU.mult).then_inc(prod_a[h], 1)
                nc.vector.tensor_tensor(pb[:, h], src[:, ::-1], kb, ALU.mult).then_inc(prod_b[h], 1)

            def khat_odd():
                dve.wait_ge(khat_mm, 2)

                def times(i, n):
                    return ps_et[:, i * P:(i + 1) * P].unsqueeze(1).broadcast_to([P, n, P])
                nc.vector.tensor_copy(khat_a[:, 2:4].rearrange("p i b d -> p (i b) d"),
                                      times(0, 2 * BPC)).then_inc(khat_odd_done, 1)
                for i, sign in enumerate((-1.0, 1.0)):
                    nc.vector.tensor_scalar(khat_b[:, 2 + i], times(1, BPC), sign, None,
                                            ALU.mult).then_inc(khat_odd_done, 1)

            def hyena(c, stage):
                light_stage(dve, nc.vector, c, stage)
                if stage.startswith("filter layer") and c == 0:
                    filter_reduce(int(stage[-1]))
                if stage == "filter fold" and c == 0:
                    filter_fold()
                if stage == "filter fold lo" and c == 0:
                    filter_fold_lo()
                if stage == "filter spectrum" and c == 0:
                    khat_odd()
                if stage == "x moments":
                    dve.wait_ge(ld_x[c], 16)
                    moments("x", c, lambda j: x_sb[:, c * TILES + j, :])
                if stage == "set-up" and c == 0:
                    dve.wait_ge(ld["cols"], 16)
                    nc.vector.tensor_scalar(fturns[:], cols_sb[:, C_FF:C_FF + 3], 0.5 / np.pi, None,
                                            ALU.mult).then_inc(fturns_done, 1)
                    tap_w2 = cols_sb[:, C_SFW:C_SFW + 9].rearrange("p (s k) -> p s k", k=3)[:, :, 2]
                    nc.vector.tensor_tensor(tap2_bias[:], tap_w2, cols_sb[:, C_BIN:C_BIN + 3],
                                            ALU.mult).then_inc(tap2_bias_a, 1)
                    dve.wait_ge(fturns_done, 1)
                    dve.wait_ge(tap2_bias_a, 1)
                    nc.vector.tensor_tensor(tap2_bias[:], tap2_bias[:], cols_sb[:, C_SFB:C_SFB + 3],
                                            ALU.add).then_inc(tap2_bias_done, 1)
                if stage == "w_in lo" and c == 0:
                    dve.wait_ge(w_in_hi_done, 1)
                    nc.vector.tensor_tensor(w_in_lo[:], w_in_sb[:], w_in_hi[:].bitcast(F32),
                                            ALU.subtract).then_inc(w_in_lo_done, 1)
                if stage == "x norm":
                    normalise("x", c, xn, lambda j: x_sb[:, c * TILES + j, :], xn_done)
                if stage == "xnT lo":
                    dve.wait_ge(xnT_hi_done, c + 1)
                    nc.vector.tensor_tensor(xnT_lo[:], ps_a[:], xnT_hi[:].bitcast(F32),
                                            ALU.subtract).then_inc(xnT_lo_done, 1)
                if stage == "x1":
                    short_conv(c, X1)
                if stage == "v":
                    short_conv(c, V)
                if stage == "x0":
                    short_conv(c, X0)
                if stage == "vT lo":
                    dve.wait_ge(vT_hi_done, c + 1)
                    nc.vector.tensor_tensor(vT_lo[:].rearrange("p k b d -> p (k b d)"), ps_a[:],
                                            vT_hi[:].rearrange("p k b d -> p (k b d)").bitcast(F32),
                                            ALU.subtract).then_inc(vT_lo_done, 1)
                if stage == "even":
                    if c == 0:
                        dve.wait_ge(khat_even_done, 3)
                    spectrum_product(c, 0, ps_b)
                if stage == "odd":
                    if c == 0:
                        dve.wait_ge(khat_odd_done, 3)
                    spectrum_product(c, 1, ps_a)
                if stage == "w_out lo" and c == 0:
                    dve.wait_ge(w_out_hi_done, 1)
                    nc.vector.tensor_tensor(w_out_lo[:], w_out_sb[:], w_out_hi[:].bitcast(F32),
                                            ALU.subtract).then_inc(w_out_lo_done, 1)
                    dve.wait_ge(router_hi_done, 1)
                    nc.vector.tensor_tensor(router_hl[:, NEXP:2 * NEXP], router_sb[:],
                                            router_hl[:, 0:NEXP].bitcast(F32),
                                            ALU.subtract).then_inc(router_lo_done, 1)
                if stage == "gated":
                    dve.wait_ge(y_mm, c + 1)
                    dve.wait_ge(uc_done[X0], c + 1)
                    if c > 0:
                        dve.wait_ge(gated_lo_done, c)
                    nc.vector.tensor_tensor(gated[:], ps_b[:], uc[X0][:].rearrange("p b t -> p (b t)"),
                                            ALU.mult).then_inc(gated_done, 1)
                if stage == "o moments":
                    dve.wait_ge(o_mm, c + 1)
                    moments("o", c, lambda j: ps_b[:, j * P:(j + 1) * P])
                if stage == "o + x":
                    if c > 1:
                        dve.wait_ge(y_done, c - 1)
                    for h in range(2):
                        t = slice(2 * h, 2 * h + 2)
                        dve.wait_ge(o_n_done, TILES * c + 2 * h + 2)
                        nc.vector.tensor_tensor(x1[:, c % 2, t], o_n[:, t], x_sb[:, c * TILES:(c + 1) * TILES, :][:, t],
                                                ALU.add).then_inc(x1_done, 1)
                        dve.wait_ge(x1_done, 2 * c + h + 1)
                        tile_stats("x1", c, (2 * h, 2 * h + 1), lambda j: x1[:, c % 2, j, :])
                    tile_moments("x1", c)
                if stage == "x1 norm":
                    normalise("x1", c, xf, lambda j: x1[:, c % 2, j, :], xf_done)
                if stage == "xfT lo":
                    dve.wait_ge(xfT_hi_done, c + 1)
                    nc.vector.tensor_tensor(xfT_lo[:, c % 2], ps_a[:], xfT_hi[:, c % 2].bitcast(F32),
                                            ALU.subtract).then_inc(xfT_lo_done, 1)
                if stage == "logits":
                    gates_a(c)
                if stage == "gates":
                    gates_b(c)

            def gates_a(c):
                dve.wait_ge(logits_mm, c + 1)
                if c > 0:
                    dve.wait_ge(gates_done, c)
                src = ps_b[:, 0:TILES * 2 * NEXP].rearrange("p (t h e) -> p t h e", t=TILES, h=2)
                rb = cols_sb[:, C_RB:C_RB + NEXP].unsqueeze(1).broadcast_to([P, TILES, NEXP])
                nc.vector.tensor_tensor(lg_a[:], src[:, :, 0, :], rb, ALU.add).then_inc(lg_a_done, 1)
                dve.wait_ge(lg_a_done, c + 1)
                nc.vector.tensor_tensor(lg[:], src[:, :, 1, :], lg_a[:], ALU.add).then_inc(lg_done, 1)
                dve.wait_ge(lg_done, c + 1)
                nc.vector.reduce_max(lg_max[:], lg[:], AX_X).then_inc(lg_max_done, 1)
                dve.wait_ge(lg_max_done, c + 1)
                nc.vector.tensor_tensor(lg_z[:], lg[:], lg_max[:].unsqueeze(2).broadcast_to([P, TILES, NEXP]),
                                        ALU.subtract).then_inc(lg_z_done, 1)

            def gates_b(c):
                full = [P, TILES, NEXP, NEXP]
                dve.wait_ge(ge_done, c + 1)
                other = ge[:].unsqueeze(2).broadcast_to(full)
                own = ge[:].unsqueeze(3).broadcast_to(full)
                flat = "p t i j -> p t (i j)"
                nc.vector.tensor_tensor(beats[:], other, own, ALU.is_gt).then_inc(beats_done, 1)
                nc.vector.tensor_tensor(ties[:], other, own, ALU.is_equal).then_inc(ties_done, 1)
                dve.wait_ge(ties_done, c + 1)
                if c == 0:
                    dve.wait_ge(ld["tri"], 16)
                nc.vector.tensor_tensor(ties_low[:].rearrange(flat), ties[:].rearrange(flat),
                                        tri_sb[:].unsqueeze(1).broadcast_to([P, TILES, NEXP * NEXP]),
                                        ALU.mult).then_inc(ties_low_done, 1)
                dve.wait_ge(beats_done, c + 1)
                dve.wait_ge(ties_low_done, c + 1)
                nc.vector.tensor_tensor(ahead[:], beats[:], ties_low[:], ALU.add).then_inc(ahead_done, 1)
                dve.wait_ge(ahead_done, c + 1)
                nc.vector.reduce_sum(place[:], ahead[:], AX_X).then_inc(place_done, 1)
                dve.wait_ge(place_done, c + 1)
                nc.vector.scalar_tensor_tensor(out=kept[:], in0=place[:], scalar=2.0, in1=ge[:],
                                               op0=ALU.is_lt, op1=ALU.mult).then_inc(kept_done, 1)
                dve.wait_ge(kept_done, c + 1)
                nc.vector.reduce_sum(ksum[:], kept[:], AX_X).then_inc(ksum_done, 1)
                dve.wait_ge(ksum_done, c + 1)
                nc.vector.reciprocal(krec[:], ksum[:]).then_inc(krec_done, 1)
                dve.wait_ge(krec_done, c + 1)
                if c > 1:
                    dve.wait_ge(weighted_done, (NEXP - 1) * (c - 1))
                nc.vector.tensor_tensor(gates[:, c % 2], kept[:],
                                        krec[:].unsqueeze(2).broadcast_to([P, TILES, NEXP]),
                                        ALU.mult).then_inc(gates_done, 1)

            def weigh_expert(n):
                c, e = divmod(n, NEXP)
                dve.wait_ge(et_mm, n + 1)
                src = ps_et[:].rearrange("p (t d) -> p t d", t=TILES)
                gate = gates[:, c % 2, :, e:e + 1].broadcast_to([P, TILES, P])
                if e == 0:
                    dve.wait_ge(gates_done, c + 1)
                    if c > 0:
                        dve.wait_ge(acc_n_done, TILES * c)
                    nc.vector.tensor_tensor(acc[:], src, gate, ALU.mult).then_inc(acc_first, 1)
                elif n == NG // FT - 1:
                    dve.wait_ge(acc_added, 3 * c + e - 1)
                    for j in range(TILES):
                        nc.vector.scalar_tensor_tensor(out=acc[:, j, :], in0=src[:, j, :],
                                                       scalar=gates[:, c % 2, j, e:e + 1], in1=acc[:, j, :],
                                                       op0=ALU.mult, op1=ALU.add).then_inc(acc_last, 1)
                else:
                    if 3 * c + e > 1:
                        dve.wait_ge(acc_added, 3 * c + e - 1)
                    nc.vector.tensor_tensor(weighted[:], src, gate, ALU.mult).then_inc(weighted_done, 1)

            for g in range(FIRST, LAST):
                if 0 <= g < NG:
                    dve.wait_ge(silu_done, g + 1)
                    dve.wait_ge(h3_mm, g + 1)
                    if g >= 2:
                        dve.wait_ge(hid_hi_done, g - 1)
                        wait_lo(dve, g - 2)
                    nc.vector.tensor_tensor(hid[:, g % 2], ps_h3[g % 2][:], silu[:, g % 2],
                                            ALU.mult).then_inc(hid_done, 1)
                for c, stage in due(DVE_AT, DVE_AHEAD, g, 0):
                    hyena(c, stage)
                if 0 <= g - 1 < NG and not by_pool(g - 1):
                    dve.wait_ge(hid_hi_done, g)
                    nc.vector.tensor_tensor(hid_lo[:, (g - 1) % 4], hid[:, (g - 1) % 2],
                                            hid_hi[:, (g - 1) % 4].bitcast(F32),
                                            ALU.subtract).then_inc(hid_lo_done, 1)
                for c, stage in due(DVE_AT, DVE_AHEAD, g, 1):
                    hyena(c, stage)
                if expert_at(g, 2) is not None:
                    weigh_expert(expert_at(g, 2))
                cc = chunk_at(g, 3)
                if cc is not None:
                    if cc < NCH - 1:
                        dve.wait_ge(acc_added, 3 * (cc + 1))
                    else:
                        dve.wait_ge(acc_last, TILES)
                    moments("moe", cc, lambda j: acc[:, j, :])
                cc = chunk_at(g, 4)
                if cc is not None and cc < NCH - 1:
                    dve.wait_ge(acc_n_done, TILES * (cc + 1))
                    nc.vector.tensor_tensor(y[:], acc_n[:], x1[:, cc % 2], ALU.add).then_inc(y_done, 1)
                if cc == NCH - 1:
                    own, acts = LAST_HALVES
                    normalise("moe", cc, acc_n, lambda j: acc[:, j, :], acc_n_last, range(TILES)[own])
                    dve.wait_ge(acc_n_last, TILES // 2)
                    nc.vector.tensor_tensor(y[:, own], acc_n[:, own], x1[:, cc % 2, own],
                                            ALU.add).then_inc(y_done, 1)
                    dve.wait_ge(acc_n_done, TILES * cc + TILES // 2)
                    nc.vector.tensor_tensor(y[:, acts], acc_n[:, acts], x1[:, cc % 2, acts],
                                            ALU.add).then_inc(y_done, 1)
                for c, stage in due(DVE_AT, DVE_AHEAD, g, 2):
                    hyena(c, stage)


def _split_table(t):
    t = t.astype(np.float32)
    bits = t.view(np.uint32).astype(np.uint64)
    bits = ((bits + 0x7FF + ((bits >> 12) & 1)) & 0xFFFFF000).astype(np.uint32)
    hi = bits.view(np.float32)
    return hi, t - hi


def _transform_tables():
    n = LFILT
    t = np.arange(SEQ, dtype=np.int64)
    even, odd = 2 * np.arange(P), 2 * np.arange(P) + 1

    def turn(f):
        return 2 * np.pi * ((t[:, None] * f[None, :]) % n) / n

    alternate = np.where(t % 2 == 0, 1.0, -1.0)
    forward = [np.cos(turn(even)), -np.sin(turn(even)), np.cos(turn(odd)), -np.sin(turn(odd))]
    forward[1][:, 0] = alternate
    inverse = [2 / n * np.cos(turn(even)).T, -2 / n * np.sin(turn(even)).T,
               2 / n * np.cos(turn(odd)).T, -2 / n * np.sin(turn(odd)).T]
    inverse[0][0] = 1 / n
    inverse[1][0] = alternate / n
    fwd = np.stack(_split_table(np.concatenate(forward, 1).reshape(2, P, LFILT)))
    inv = np.stack(_split_table(np.stack(inverse)))
    return (np.ascontiguousarray(fwd.transpose(2, 0, 1, 3)), np.ascontiguousarray(inv.transpose(2, 0, 1, 3)))


def _filter_tables():
    t = np.linspace(0.0, 1.0, LFILT).astype(np.float32)
    w = (2.0 * np.pi * np.arange(LFILT) / LFILT).astype(np.float32)
    fw = (np.float32(1e-4) * w).astype(np.float64)
    z = np.stack([t, np.cos(fw), -np.sin(fw)]).astype(np.float32)
    deltas = np.linspace(np.log(0.01) / 1.5, np.log(0.01) / 0.3, P)
    window = np.exp(-t[:, None].astype(np.float64) * np.abs(deltas)[None, :]) + 0.05
    return z, window.astype(np.float32)


def kernel(**inputs):
    import concourse.bacc as _bacc
    from concourse.bass_utils import run_bass_kernel_spmd as _run

    d = {k.removeprefix("L0_"): np.asarray(v) for k, v in inputs.items()}
    u = d["attn_u"]
    x = np.ascontiguousarray(u.reshape(-1, P))
    z, window = _filter_tables()
    fwd, inv = _transform_tables()
    half = P // 2

    def twice(v):
        return np.concatenate([v, v])[:, None]

    cols = np.concatenate(
        [d["attn_b_in"].reshape(3, P).T,
         d["attn_sf_w"].reshape(3, P, 3).transpose(1, 0, 2).reshape(P, 9),
         d["attn_sf_b"].reshape(3, P).T,
         *(twice(d[f"attn_f_b{n}"]) for n in (1, 2, 3)),
         *(twice(d[f"attn_freq{n}"]) for n in (1, 2, 3)),
         np.broadcast_to(d["ffn_router_b"], (P, NEXP)), d["attn_b_out"][:, None]], axis=1)
    filt_z = np.zeros((6, P + SEQ), np.float32)
    filt_mats = np.zeros((P, 3, P), np.float32)
    for h in range(2):
        a = slice(h * half, (h + 1) * half)
        filt_z[3 * h:3 * h + 3, a] = d["attn_f_w1"]
        filt_z[3 * h:3 * h + 3, P:] = z[:, h * SEQ:(h + 1) * SEQ]
        filt_mats[a, 0, a] = d["attn_f_w2"]
        filt_mats[a, 1, a] = d["attn_f_w3"]
        filt_mats[a, 2, :] = d["attn_f_wout"]
    arrays = {
        "x": x, "w_in": d["attn_w_in"], "w_out": d["attn_w_out"], "cols": cols, "fbias": d["attn_filt_bias"][None, :],
        "filt_z": filt_z, "filt_mats": filt_mats,
        "decay": np.ascontiguousarray(window.reshape(4, P, P).transpose(1, 0, 2)),
        "router": d["ffn_router_w"], "w1": d["ffn_w1"], "w3": d["ffn_w3"], "w2": d["ffn_w2"],
        "fwd": fwd, "inv": inv, "ident": np.eye(P, dtype=np.float32),
        "tri": np.ascontiguousarray(np.broadcast_to(np.tril(np.ones((NEXP, NEXP), np.float32), -1).reshape(1, -1),
                                                    (P, NEXP * NEXP))),
    }
    nc = _bacc.Bacc("TRN2", target_bir_lowering=False, num_devices=1)
    ins, args = {}, {}
    for name, a in arrays.items():
        a = np.ascontiguousarray(a)
        ins[f"in_{name}"] = a
        args[name] = nc.dram_tensor(f"in_{name}", a.shape, mybir.dt.from_np(a.dtype), kind="ExternalInput").ap()
    out = nc.dram_tensor("out_x", x.shape, F32, kind="ExternalOutput").ap()
    build(nc, out=out, **args)
    got = _run(nc, [ins], core_ids=[0]).results[0]["out_x"]
    return got.reshape(u.shape)
```
